# Optimizing a Trainium2 kernel written in Bass

```python
import numpy as np
import jax
import jax.numpy as jnp

def _softmax(x, axis=-1):
    return jax.nn.softmax(x, axis=axis)

def _gelu(x):
    return jax.nn.gelu(x, approximate=True)

def _silu(x):
    return jax.nn.silu(x)

def _sigmoid(x):
    return jax.nn.sigmoid(x)

def _layernorm(x, axis=-1, eps=1e-05):
    m = jnp.mean(x, axis=axis, keepdims=True)
    v = jnp.var(x, axis=axis, keepdims=True)
    return (x - m) / jnp.sqrt(v + eps)

def _scatter_add(tgt, idx, src, axis=0):
    return tgt.at[idx].add(src)

def _segment_sum(src, seg, n):
    return jax.ops.segment_sum(src, seg, n)
kernel_name = 'mk_xattn_ffn_d1_seqx_r4_323383'

def setup_inputs(seed: int=0):
    np.random.seed(seed)
    _w = jnp.asarray

    def _rec_inputs():
        import jax
        import jax.numpy as jnp
        _rk = jax.random.key(seed)
        x = 7.22e-05 + 1 * jax.random.normal(jax.random.fold_in(_rk, 1), (8, 256, 256), jnp.float32)
        _lenS = 256 - jax.random.randint(jax.random.fold_in(_rk, 7), (8,), 0, max(1, 256 // 4) + 1, jnp.int32)
        _lenS2 = 256 - jax.random.randint(jax.random.fold_in(_rk, 8), (8,), 0, max(1, 256 // 4) + 1, jnp.int32)
        _ctx_1024P = jax.random.normal(jax.random.fold_in(_rk, 11), (8, 16, 256), jnp.float32)
        _ctx_1024c = jax.random.dirichlet(jax.random.fold_in(_rk, 511), 0.3 * jnp.ones((16,), jnp.float32), (8, 256))
        _ctx_1024t = jnp.einsum('bsk,bkd->bsd', _ctx_1024c, _ctx_1024P)
        _ctx_1024t = _ctx_1024t * jax.lax.rsqrt(jnp.mean(jnp.square(_ctx_1024t)) + 1e-12) * 0.953939
        ctx_1024 = 4.13588e-05 + 0.999923 * (_ctx_1024t + 0.3 * jax.random.normal(jax.random.fold_in(_rk, 611), (8, 256, 256), jnp.float32))
        _validS = jnp.arange(256)[None, :] < _lenS[:, None]
        _validS2 = jnp.arange(256)[None, :] < _lenS2[:, None]
        _causal = jnp.tril(jnp.ones((256, 256), dtype=bool))
        mask_BxS2_bf1 = jnp.ones((8, 256), dtype=bool)
        mask_BxSxS2_bf1 = jnp.ones((8, 256, 256), dtype=bool)
        return (x, ctx_1024, mask_BxS2_bf1, mask_BxSxS2_bf1)
    x, ctx_1024, mask_BxS2_bf1, mask_BxSxS2_bf1 = _rec_inputs()

    def _L0_xattn_setup():
        import jax, jax.numpy as jnp
        import numpy as np
        N, L, E, H = (4, 512, 256, 16)
        D = E // H
        key = jax.random.key(seed)
        ks = jax.random.split(key, 8)
        s = 1.0 / np.sqrt(E)
        return {'Q': jax.random.normal(ks[0], (N, L, E), jnp.float32), 'K': jax.random.normal(ks[1], (N, L, E), jnp.float32), 'V': jax.random.normal(ks[2], (N, L, E), jnp.float32), 'Wq': jax.random.normal(ks[3], (E, E), jnp.float32) * s, 'Wk': jax.random.normal(ks[4], (E, E), jnp.float32) * s, 'Wv': jax.random.normal(ks[5], (E, E), jnp.float32) * s, 'Wo': jax.random.normal(ks[6], (E, E), jnp.float32) * s, 'bo': jax.random.normal(ks[7], (E,), jnp.float32) * s, 'padding_mask': jnp.ones((N, L), dtype=bool), 'attention_mask': jnp.ones((N, L, L), dtype=bool)}
    _L0_xattn_all = _L0_xattn_setup()
    _L0_xattn_in = {k: v for k, v in _L0_xattn_all.items() if k in ('Wq', 'Wk', 'Wv', 'Wo', 'bo')}
    del _L0_xattn_all

    def _L0_ffn_setup():
        import jax, jax.numpy as jnp
        import numpy as np
        D_MODEL = 256
        N_HEAD = 16
        HEAD_DIM = D_MODEL // N_HEAD
        D_FF = 1024
        N_EXPERTS = 4
        EPS = 1e-05

        def _layer_norm(x, gamma, beta):
            mu = jnp.mean(x, axis=-1, keepdims=True)
            var = jnp.mean((x - mu) ** 2, axis=-1, keepdims=True)
            return (x - mu) / jnp.sqrt(var + EPS) * gamma + beta
        key = jax.random.key(seed)
        ks = jax.random.split(key, 20)
        f32 = jnp.float32
        sc = 1.0 / np.sqrt(D_MODEL)
        scf = 1.0 / np.sqrt(D_FF)
        return {'src': jax.random.normal(ks[0], (4, 128, D_MODEL), f32), 'Wq': jax.random.normal(ks[1], (D_MODEL, D_MODEL), f32) * sc, 'bq': jnp.zeros((D_MODEL,), f32), 'Wk': jax.random.normal(ks[2], (D_MODEL, D_MODEL), f32) * sc, 'bk': jnp.zeros((D_MODEL,), f32), 'Wv': jax.random.normal(ks[3], (D_MODEL, D_MODEL), f32) * sc, 'bv': jnp.zeros((D_MODEL,), f32), 'Wo': jax.random.normal(ks[4], (D_MODEL, D_MODEL), f32) * sc, 'bo': jnp.zeros((D_MODEL,), f32), 'router_w': jax.random.normal(ks[5], (D_MODEL, 1), f32) * 0.05, 'router_b': jnp.zeros((1,), f32), 'W1': jax.random.normal(ks[6], (N_EXPERTS, D_MODEL, D_FF), f32) * sc, 'b1': jnp.zeros((N_EXPERTS, D_FF), f32), 'W2': jax.random.normal(ks[7], (N_EXPERTS, D_FF, D_MODEL), f32) * scf, 'b2': jnp.zeros((N_EXPERTS, D_MODEL), f32), 'ln1_g': jnp.ones((D_MODEL,), f32), 'ln1_b': jnp.zeros((D_MODEL,), f32), 'ln2_g': jnp.ones((D_MODEL,), f32), 'ln2_b': jnp.zeros((D_MODEL,), f32)}
    _L0_ffn_all = _L0_ffn_setup()
    _L0_ffn_in = {k: v for k, v in _L0_ffn_all.items() if k in ('Wq', 'bq', 'Wk', 'bk', 'Wv', 'bv', 'Wo', 'bo', 'router_w', 'router_b', 'W1', 'b1', 'W2', 'b2', 'ln1_g', 'ln1_b', 'ln2_g', 'ln2_b')}
    del _L0_ffn_all
    return {'x': x, 'ctx_1024': ctx_1024, 'mask_BxS2_bf1': mask_BxS2_bf1, 'mask_BxSxS2_bf1': mask_BxSxS2_bf1, 'L0_xattn_Wq': _L0_xattn_in['Wq'], 'L0_xattn_Wk': _L0_xattn_in['Wk'], 'L0_xattn_Wv': _L0_xattn_in['Wv'], 'L0_xattn_Wo': _L0_xattn_in['Wo'], 'L0_xattn_bo': _L0_xattn_in['bo'], 'L0_ffn_Wq': _L0_ffn_in['Wq'], 'L0_ffn_bq': _L0_ffn_in['bq'], 'L0_ffn_Wk': _L0_ffn_in['Wk'], 'L0_ffn_bk': _L0_ffn_in['bk'], 'L0_ffn_Wv': _L0_ffn_in['Wv'], 'L0_ffn_bv': _L0_ffn_in['bv'], 'L0_ffn_Wo': _L0_ffn_in['Wo'], 'L0_ffn_bo': _L0_ffn_in['bo'], 'L0_ffn_router_w': _L0_ffn_in['router_w'], 'L0_ffn_router_b': _L0_ffn_in['router_b'], 'L0_ffn_W1': _L0_ffn_in['W1'], 'L0_ffn_b1': _L0_ffn_in['b1'], 'L0_ffn_W2': _L0_ffn_in['W2'], 'L0_ffn_b2': _L0_ffn_in['b2'], 'L0_ffn_ln1_g': _L0_ffn_in['ln1_g'], 'L0_ffn_ln1_b': _L0_ffn_in['ln1_b'], 'L0_ffn_ln2_g': _L0_ffn_in['ln2_g'], 'L0_ffn_ln2_b': _L0_ffn_in['ln2_b']}

def reference(x, ctx_1024, mask_BxS2_bf1, mask_BxSxS2_bf1, L0_xattn_Wq, L0_xattn_Wk, L0_xattn_Wv, L0_xattn_Wo, L0_xattn_bo, L0_ffn_Wq, L0_ffn_bq, L0_ffn_Wk, L0_ffn_bk, L0_ffn_Wv, L0_ffn_bv, L0_ffn_Wo, L0_ffn_bo, L0_ffn_router_w, L0_ffn_router_b, L0_ffn_W1, L0_ffn_b1, L0_ffn_W2, L0_ffn_b2, L0_ffn_ln1_g, L0_ffn_ln1_b, L0_ffn_ln2_g, L0_ffn_ln2_b):
    import jax
    import jax.numpy as jnp

    def _L0_xattn_ref(Q, K, V, Wq, Wk, Wv, Wo, bo, padding_mask, attention_mask):
        import jax, jax.numpy as jnp
        import numpy as np
        N, L, E, H = (4, 512, 256, 16)
        D = E // H
        n, lq, e = Q.shape
        q = jnp.einsum('nle,fe->nlf', Q, Wq).reshape(n, lq, H, D).transpose(0, 2, 1, 3)
        k = jnp.einsum('nle,fe->nlf', K, Wk).reshape(n, -1, H, D).transpose(0, 2, 1, 3)
        v = jnp.einsum('nle,fe->nlf', V, Wv).reshape(n, -1, H, D).transpose(0, 2, 1, 3)
        attn = jnp.einsum('nhqd,nhkd->nhqk', q, k) / jnp.sqrt(jnp.asarray(D, q.dtype))
        neg_inf = jnp.asarray(-jnp.inf, attn.dtype)
        attn = jnp.where(padding_mask[:, None, :, None], attn, neg_inf)
        attn = jnp.where(attention_mask[:, None], attn, neg_inf)
        p = jax.nn.softmax(attn, axis=-1)
        out = jnp.einsum('nhqk,nhkd->nhqd', p, v)
        out = out.transpose(0, 2, 1, 3).reshape(n, lq, e)
        return jnp.einsum('nle,fe->nlf', out, Wo) + bo

    def _L0_ffn_ref(src, Wq, bq, Wk, bk, Wv, bv, Wo, bo, router_w, router_b, W1, b1, W2, b2, ln1_g, ln1_b, ln2_g, ln2_b):
        import jax, jax.numpy as jnp
        import numpy as np
        D_MODEL = 256
        N_HEAD = 16
        HEAD_DIM = D_MODEL // N_HEAD
        D_FF = 1024
        N_EXPERTS = 4
        EPS = 1e-05

        def _layer_norm(x, gamma, beta):
            mu = jnp.mean(x, axis=-1, keepdims=True)
            var = jnp.mean((x - mu) ** 2, axis=-1, keepdims=True)
            return (x - mu) / jnp.sqrt(var + EPS) * gamma + beta
        B, T, _ = src.shape
        q = (src @ Wq + bq).reshape(B, T, N_HEAD, HEAD_DIM)
        k = (src @ Wk + bk).reshape(B, T, N_HEAD, HEAD_DIM)
        v = (src @ Wv + bv).reshape(B, T, N_HEAD, HEAD_DIM)
        scale = HEAD_DIM ** (-0.5)
        scores = jnp.einsum('bqhd,bkhd->bhqk', q, k) * scale
        probs = jax.nn.softmax(scores, axis=-1)
        attn = jnp.einsum('bhqk,bkhd->bqhd', probs, v).reshape(B, T, D_MODEL)
        attn = attn @ Wo + bo
        x = _layer_norm(src + attn, ln1_g, ln1_b)
        keys = (x @ router_w + router_b)[..., 0]
        expert_idx = jnp.remainder(jnp.floor(keys).astype(jnp.int32), N_EXPERTS)
        ff_out = jnp.zeros_like(x)
        for e in range(N_EXPERTS):
            h = jax.nn.relu(x @ W1[e] + b1[e])
            y = h @ W2[e] + b2[e]
            ff_out = ff_out + jnp.where((expert_idx == e)[..., None], y, 0.0)
        return _layer_norm(x + ff_out, ln2_g, ln2_b)
    x = x + _L0_xattn_ref(_layernorm(x, axis=-1), ctx_1024, ctx_1024, L0_xattn_Wq, L0_xattn_Wk, L0_xattn_Wv, L0_xattn_Wo, L0_xattn_bo, mask_BxS2_bf1, mask_BxSxS2_bf1)
    x = x + _L0_ffn_ref(_layernorm(x, axis=-1), L0_ffn_Wq, L0_ffn_bq, L0_ffn_Wk, L0_ffn_bk, L0_ffn_Wv, L0_ffn_bv, L0_ffn_Wo, L0_ffn_bo, L0_ffn_router_w, L0_ffn_router_b, L0_ffn_W1, L0_ffn_b1, L0_ffn_W2, L0_ffn_b2, L0_ffn_ln1_g, L0_ffn_ln1_b, L0_ffn_ln2_g, L0_ffn_ln2_b)
    return x

_drawn_inputs = setup_inputs


def setup_inputs(seed=0):
    import zlib

    import numpy as np

    out = dict(_drawn_inputs(seed))
    spreads = {'L0_ffn_bq': (0.0, 0.292),
     'L0_ffn_bk': (0.0, 0.8),
     'L0_ffn_bv': (0.0, 0.1),
     'L0_ffn_bo': (0.0, 0.1),
     'L0_ffn_b1': (0.0, 0.291),
     'L0_ffn_b2': (0.0, 0.1),
     'L0_ffn_ln1_g': (1.0, 0.2),
     'L0_ffn_ln1_b': (0.0, 0.1),
     'L0_ffn_ln2_g': (1.0, 0.2),
     'L0_ffn_ln2_b': (0.0, 0.1)}
    factors = {}
    for name, (base, spread) in spreads.items():
        noise = np.random.default_rng([zlib.crc32(name.encode()), seed]).standard_normal(out[name].shape)
        drawn = base * np.exp(spread * noise) if base else spread * noise
        out[name] = jnp.asarray(drawn.astype(out[name].dtype))
    for name, factor in factors.items():
        out[name] = (out[name] * factor).astype(out[name].dtype)
    return out
```

```python
import numpy as np
import concourse.bass as bass
from concourse import mybir
from contextlib import ExitStack

F32 = mybir.dt.float32
BF16 = mybir.dt.bfloat16
U8 = mybir.dt.uint8
I32 = mybir.dt.int32
ALU = mybir.AluOpType
ACT = mybir.ActivationFunctionType
AX = mybir.AxisListType

P = 128
BATCH, SEQ, E = 8, 256, 256
HEADS, HD = 16, 16
DFF, EXPERTS = 1024, 4
TT = SEQ // P
KC = E // P
GROUPS, GH = 4, 4
TERMS = 6
SHIFT_ROW = TERMS * HD
Q_PARTS = ((0, 0), (1, 0), (2, 0), (3, 1), (4, 1), (5, 2))
K_LOADS = ((0, 0, 3), (3, 0, 2), (5, 0, 1))
SCALE = float(HD) ** -0.5
EPS = 1e-5
MASKED = 1e30
CREDIT = 2
MC = DFF // P
VECS = ("bo0", "bv1", "bo1", "ln1g", "ln1b", "ln2g", "ln2b", "rw", "b2_0", "b2_1", "b2_2", "b2_3")


def build(nc, io):
    ctx = ExitStack()
    with ctx:
        def sb(name, shape, dt=F32):
            return ctx.enter_context(nc.sbuf_tensor(name, shape, dt))

        def sem(name):
            return ctx.enter_context(nc.semaphore(name))

        def dram(name, shape, dt):
            return nc.dram_tensor(name, shape, dt, kind="Internal").ap()

        w_attn = sb("w_attn", [P, 8, KC, E])
        vec = sb("vec", [P, len(VECS), E])
        ident = sb("ident", [P, P])
        ident_bf = sb("ident_bf", [P, P], BF16)
        bias_qk = sb("bias_qk", [P, 2, KC])
        b1_sb = sb("b1_sb", [P, EXPERTS * MC])
        rb_sb = sb("rb_sb", [P, 1])
        pad_sb = sb("pad_sb", [P, BATCH * TT], U8)
        w1 = sb("w1", [P, EXPERTS, KC, DFF])
        w2 = sb("w2", [P, EXPERTS, MC, E])
        flat = w1[:, :, :, :].rearrange("p a b c -> p (a b c)")
        SLOT = TT * E

        def view(n, slots):
            return flat[:, n * SLOT:(n + slots) * SLOT]

        xb = view(0, 2).rearrange("p (s t e) -> p s t e", s=2, t=TT)
        cb = view(2, 2).rearrange("p (s t e) -> p s t e", s=2, t=TT)
        xT = view(4, 2).rearrange("p (s t e) -> p s t e", s=2, t=KC)
        cT = view(6, 2).rearrange("p (s t e) -> p s t e", s=2, t=KC)
        full = view(8, 2).rearrange("p (s t e) -> p s t e", s=2, t=KC)
        rest = view(10, 2).rearrange("p (s t e) -> p s t e", s=2, t=KC)
        parts = view(12, 3).bitcast(BF16).rearrange("p (o r t e) -> p o r t e", o=2, r=3, t=KC)
        mask_u8 = sb("mask_u8", [P, 2, TT, SEQ], U8)

        src_all = sb("src_all", [P, BATCH * TT, E])
        v_all = sb("v_all", [P, BATCH * TT, E])
        bias_all = sb("bias_all", [P, BATCH * TT, SEQ], BF16)
        seen = sb("seen", [P, BATCH * TT])
        nan_all = sb("nan_all", [P, BATCH * TT])
        stack_q = sb("stack_q", [P, HEADS, SEQ], BF16)
        stack_k = sb("stack_k", [P, HEADS, SEQ], BF16)
        probs = sb("probs", [P, 2, GH, TT * SEQ])
        v_ones = sb("v_ones", [P, TT, HEADS, 2 * HD])
        negmax = sb("negmax", [P, GH * TT], BF16)
        negmax_t = sb("negmax_t", [GH * TT, P], BF16)
        o_raw = sb("o_raw", [P, SEQ])
        rden = sb("rden", [P, TT, GH])
        o_norm = sb("o_norm", [P, TT, E])
        o_t = sb("o_t", [P, KC, SEQ])
        xres = sb("xres", [P, TT, E])
        resid = sb("resid", [P, TT, E])
        stats = sb("stats", [P, TT, 6])
        mv = sb("mv", [P, TT, 2])
        rstd = sb("rstd", [P, TT])
        var_eps = sb("var_eps", [P, TT])
        neg_half = sb("neg_half", [P, TT])
        keys_b = sb("keys_b", [P, TT])
        keys = sb("keys", [P, BATCH * TT])
        route = sb("route", [P, 6, BATCH * TT])
        route_i = sb("route_i", [P, BATCH * TT], I32)
        onehot = sb("onehot", [P, EXPERTS, BATCH * TT])
        hidden = probs[:, :, :, :].rearrange("p s a (b t) -> p s (a b) t", b=2)
        x2T = o_t
        bias_q_scaled = sb("bias_q_scaled", [P, KC])
        x2s = sb("x2s", [P, TT, E])
        ff = o_norm

        bank = [ctx.enter_context(nc.psum_tensor(f"bank{i}", [P, 512], F32)) for i in range(8)]

        q_dram = dram("q_parts", [2 * BATCH, 3, HD, HEADS, SEQ], BF16)
        k_dram = dram("k_parts", [2 * BATCH, 3, HD, HEADS, SEQ], BF16)
        x1_dram = dram("x1_keep", [BATCH * SEQ, E], F32)

        s_const = sem("constants_loaded")
        s_ident = sem("ident_bf_ready")
        s_ones = sem("ones_ready")
        s_wts = sem("ffn_weights_loaded")
        s_xin = [sem(f"x_loaded{s}") for s in range(2)]
        s_cin = [sem(f"ctx_loaded{s}") for s in range(2)]
        s_min = [sem(f"mask_loaded{s}") for s in range(2)]
        s_bias = sem("mask_bias_ready")
        s_nan = sem("nan_ready")
        s_stats, s_aggr, s_rstd, s_ln = sem("stats_done"), sem("aggr_done"), sem("rstd_done"), sem("ln_done")
        s_tx, s_tc = sem("x_transposed"), sem("ctx_transposed")
        s_xT, s_cT = sem("xT_ready"), sem("cT_ready")
        s_proj = {o: sem(f"{o}_projected") for o in "qkv"}
        s_full = {o: sem(f"{o}_full_ready") for o in "qk"}
        s_hi = {o: sem(f"{o}_hi_ready") for o in "qk"}
        s_rest = {o: sem(f"{o}_rest_ready") for o in "qk"}
        s_mid = {o: sem(f"{o}_mid_ready") for o in "qk"}
        s_lo = {o: sem(f"{o}_lo_ready") for o in "qk"}
        s_stored = {o: sem(f"{o}_parts_stored") for o in "qk"}
        s_v = sem("v_ready")
        s_stack = [sem(f"stack_loaded{g}") for g in range(GROUPS)]
        s_row = sem("shift_row_loaded")
        s_vones = sem("v_ones_ready")
        s_mm = sem("max_scores_ready")
        s_max = sem("max_taken")
        s_nt = sem("negmax_transposed")
        s_ntc = sem("negmax_t_ready")
        s_sc = sem("scores_ready")
        s_exp = sem("probs_ready")
        s_pv = sem("pv_done")
        s_oraw = sem("o_raw_ready")
        s_ot = sem("o_raw_transposed")
        s_rden = sem("rden_ready")
        s_on = sem("o_norm_ready")
        s_t2 = sem("o_norm_transposed")
        s_oT = sem("o_t_ready")
        s_wo = sem("out_projected")
        s_xres = sem("xres_loaded")
        s_res = sem("resid_ready")
        s_x1 = sem("x1_ready")
        s_x1st = sem("x1_stored")
        s_end = sem("attention_batch_done")
        s_vareps = sem("var_eps_ready")
        s_gate = sem("stats_gate")
        s_step = sem("vector_step")
        s_keys = sem("router_keys_ready")
        s_fx = sem("ffn_x_transposed")
        s_fxT = sem("ffn_xT_ready")
        s_h = sem("hidden_psum_ready")
        s_ha = [sem("hidden_by_scalar"), sem("hidden_by_vector")]
        s_y = sem("expert_out_ready")
        s_yt = sem("expert_out_taken")
        s_step2 = sem("ffn_step")
        s_x1in = sem("x1_loaded")
        s_outr = sem("out_ready")
        s_src, s_x2s = sem("src_staged"), sem("x2_staged")
        s_y1, s_y2 = sem("ln1_scaled"), sem("x2_ready")
        s_f1, s_f2 = sem("ln2_scaled"), sem("ln2_shifted")
        s_out = sem("out_stored")

        x_d, c_d, m_d, out_d = io["x"], io["ctx"], io["mask"], io["out"]
        OPS = {"q": 0, "k": 1}
        V = {n: vec[:, i, :] for i, n in enumerate(VECS)}
        block = ctx.enter_context(nc.Block())

        def tiles(b):
            return slice(b * TT, b * TT + TT) if isinstance(b, int) else bass.ds(b * TT, TT)

        def rows(b):
            return slice(b * SEQ, b * SEQ + SEQ) if isinstance(b, int) else bass.ds(b * SEQ, SEQ)

        @block.sync
        def _(sp):
            sp.dma_start(w_attn[:, :, :, :], io["w_attn"].rearrange("n (c p) e -> p n c e", p=P)).then_inc(s_const, 16)
            sp.dma_start(ident[:, :], io["ident"]).then_inc(s_const, 16)
            sp.dma_start(vec[:, :, :], io["vec"].partition_broadcast(P)).then_inc(s_const, 16)
            sp.dma_start(bias_qk[:, :, :], io["bias_qk"]).then_inc(s_const, 16)
            sp.dma_start(b1_sb[:, :], io["b1"]).then_inc(s_const, 16)
            sp.dma_start(rb_sb[:, :], io["rb"].partition_broadcast(P)).then_inc(s_const, 16)
            sp.dma_start(pad_sb[:, :], io["pad"]).then_inc(s_const, 16)

            def load_inputs(b, s):
                sp.dma_start(xb[:, s, :, :], x_d[rows(b), :].rearrange("(t p) e -> p t e", p=P)).then_inc(s_xin[s], 16)
                sp.dma_start(cb[:, s, :, :], c_d[rows(b), :].rearrange("(t p) e -> p t e", p=P)).then_inc(s_cin[s], 16)
                sp.dma_start(mask_u8[:, s, :, :], m_d[rows(b), :].rearrange("(t p) e -> p t e", p=P)).then_inc(s_min[s], 16)

            def store_parts(B):
                for o in "qk":
                    sp.wait_ge(s_mid[o], B + 1)
                    sp.wait_ge(s_lo[o], B + 1)
                    dst = (q_dram if o == "q" else k_dram)[B]
                    sp.dma_start(dst.rearrange("r (t d) h k -> (d h) r t k", t=KC), parts[:, OPS[o], :, :, :]).then_inc(s_stored[o], 16)

            def load_stack(B, g):
                hs = slice(GH * g, GH * g + GH)
                for r, part in Q_PARTS:
                    if r in (0, 3, 5):
                        n = {0: 3, 3: 2, 5: 1}[r]
                        src = q_dram[B, part, :, hs, :]
                        for j in range(n):
                            sp.dma_start(stack_q[HD * (r + j):HD * (r + j + 1), hs, :], src).then_inc(s_stack[g], 16)
                for r, p0, n in K_LOADS:
                    sp.dma_start(stack_k[HD * r:HD * (r + n), hs, :],
                                 k_dram[B, p0:p0 + n, :, hs, :].rearrange("r d h k -> (r d) h k")).then_inc(s_stack[g], 16)

            def shift_row(U, g):
                sp.wait_ge(s_ntc, U + 1)
                sp.dma_start(stack_q[SHIFT_ROW:SHIFT_ROW + 1, GH * g:GH * g + GH, :].rearrange("o h (t k) -> o (h t) k", t=TT),
                             negmax_t[:, :]).then_inc(s_row, 16)

            def load_xres(b):
                sp.dma_start(xres[:, :, :], x_d[rows(b), :].rearrange("(t p) e -> p t e", p=P)).then_inc(s_xres, 16)

            for s in range(2):
                load_inputs(s, s)
            with sp.Fori(0, BATCH // 2 - 1) as p:
                for s in range(2):
                    b = 2 * p + s
                    store_parts(b)
                    sp.wait_ge(s_tx, b + 1)
                    sp.wait_ge(s_tc, b + 1)
                    sp.wait_ge(s_bias, b + 1)
                    load_inputs(b + 2, s)
            for b in (BATCH - 2, BATCH - 1):
                store_parts(b)

            for a in range(2):
                if a == 1:
                    with sp.Fori(0, BATCH) as b:
                        store_parts(b + BATCH)
                    for o in "qk":
                        sp.wait_ge(s_stored[o], 16 * 2 * BATCH)
                    sp.wait_ge(s_proj["v"], CREDIT + 2 * BATCH)
                    sp.dma_start(w1[:, :, :, :], io["w1"].rearrange("n (c p) f -> p n c f", p=P)).then_inc(s_wts, 16)
                    sp.dma_start(w2[:, :, :, :], io["w2"].rearrange("n (c p) e -> p n c e", p=P)).then_inc(s_wts, 16)
                B0 = a * BATCH
                for o in "qk":
                    sp.wait_ge(s_stored[o], 16 * (B0 + 1))
                for g in range(GROUPS):
                    load_stack(B0, g)
                if a == 0:
                    load_xres(0)
                for g in range(2):
                    shift_row(4 * B0 + g, g)

                def batch(b, last):
                    B = b + B0
                    for g in range(GROUPS):
                        U = 4 * B + g
                        if not (last and g >= 2):
                            shift_row(U + 2, (g + 2) % GROUPS)
                        if not last:
                            if g == 0:
                                for o in "qk":
                                    sp.wait_ge(s_stored[o], 16 * (B + 2))
                            sp.wait_ge(s_sc, GH * (U + 1))
                            load_stack(B + 1, g)
                    if a == 0:
                        if not last:
                            sp.wait_ge(s_res, B + 1)
                            load_xres(b + 1)
                        sp.wait_ge(s_x1, B + 1)
                        sp.dma_start(x1_dram[rows(b), :].rearrange("(t p) e -> p t e", p=P), resid[:, :, :]).then_inc(s_x1st, 16)

                with sp.Fori(0, BATCH - 1) as b:
                    batch(b, False)
                batch(BATCH - 1, True)

            sp.wait_ge(s_x1st, 16 * BATCH)
            sp.wait_ge(s_end, 2 * BATCH)
            sp.dma_start(xres[:, :, :], x1_dram[rows(0), :].rearrange("(t p) e -> p t e", p=P)).then_inc(s_x1in, 16)

            def finish(b, last):
                sp.wait_ge(s_outr, b + 1)
                sp.dma_start(out_d[rows(b), :].rearrange("(t p) e -> p t e", p=P), resid[:, :, :]).then_inc(s_out, 16)
                if not last:
                    sp.dma_start(xres[:, :, :], x1_dram[rows(b + 1), :].rearrange("(t p) e -> p t e", p=P)).then_inc(s_x1in, 16)

            with sp.Fori(0, BATCH - 1) as b:
                finish(b, False)
            finish(BATCH - 1, True)
            sp.wait_ge(s_out, 16 * BATCH)

        @block.tensor
        def _(pe):
            mm = nc.tensor.matmul
            pe.wait_ge(s_const, 16 * 7)
            pe.wait_ge(s_ident, 1)

            def turn(dst, src):
                for c in range(KC):
                    for t in range(TT):
                        last = nc.tensor.transpose(dst[:, c * SEQ + t * P:c * SEQ + (t + 1) * P], src[:, t, c * P:(c + 1) * P], ident[:, :])
                return last

            def project_t(dst, w, xt):
                for t in range(KC):
                    for c in range(KC):
                        last = mm(dst[:, t * SEQ:(t + 1) * SEQ], w_attn[:, w, c, t * P:(t + 1) * P], xt[:, c, :],
                                  start=(c == 0), stop=(c == KC - 1))
                return last

            def project(dst, w, xt):
                for t in range(TT):
                    for c in range(KC):
                        last = mm(dst[:, t * E:(t + 1) * E], xt[:, c, t * P:(t + 1) * P], w_attn[:, w, c, :],
                                  start=(c == 0), stop=(c == KC - 1))
                return last

            def projections(a, p):
                for s in range(2):
                    b = 2 * p + s
                    B = b + a * BATCH
                    if a == 0:
                        pe.wait_ge(s_ln, B + 1)
                        pe.wait_ge(s_xT, B)
                        turn(bank[s], xb[:, s, :, :]).then_inc(s_tx, 1)
                        pe.wait_ge(s_cin[s], 16 * p + 16)
                        pe.wait_ge(s_cT, B)
                        turn(bank[2 + s], cb[:, s, :, :]).then_inc(s_tc, 1)
                    else:
                        pe.wait_ge(s_src, b + 1)
                        pe.wait_ge(s_xT, B)
                        turn(bank[s], xb[:, s, :, :]).then_inc(s_tx, 1)
                for s in range(2):
                    B = 2 * p + s + a * BATCH
                    src = xT if a else cT
                    pe.wait_ge(s_xT, B + 1)
                    pe.wait_ge(s_hi["q"], B)
                    project_t(bank[4], 4 * a, xT[:, s, :, :]).then_inc(s_proj["q"], 1)
                    if a == 0:
                        pe.wait_ge(s_cT, B + 1)
                    pe.wait_ge(s_hi["k"], B)
                    project_t(bank[5], 4 * a + 1, src[:, s, :, :]).then_inc(s_proj["k"], 1)
                    pe.wait_ge(s_v, B)
                    project(bank[6], 4 * a + 2, src[:, s, :, :]).then_inc(s_proj["v"], 1)

            def max_scores(U, g, i, b, a):
                h, n = GH * g + i, GH * U + i
                if i == 0:
                    pe.wait_ge(s_stack[g], 16 * 9 * (b + a * BATCH + 1))
                if not isinstance(n, int) or n >= 2:
                    pe.wait_ge(s_max, n - 1)
                for t in range(TT):
                    dst = bank[i % 2][:, t * SEQ:(t + 1) * SEQ]
                    last = mm(dst, stack_q[0:SHIFT_ROW, h, t * P:(t + 1) * P], stack_k[0:SHIFT_ROW, h, :],
                              start=True, stop=(a == 1))
                    if a == 0:
                        last = mm(dst, ident_bf[:, :], bias_all[:, b * TT + t, :], start=False, stop=True)
                last.then_inc(s_mm, 1)

            def turn_max(U):
                pe.wait_ge(s_max, GH * (U + 1))
                pe.wait_ge(s_ntc, U)
                nc.tensor.transpose(bank[5][0:GH * TT, 0:P // 2].bitcast(BF16), negmax[:, :], ident_bf[:, :]).then_inc(s_nt, 1)

            def scores(U, g, i, b, a):
                h, n = GH * g + i, GH * U + i
                if i == 0:
                    pe.wait_ge(s_row, 16 * (U + 1))
                pe.wait_ge(s_exp, CREDIT + n - 1)
                for k in range(TT):
                    dst = bank[2 + i % 2][:, k * SEQ:(k + 1) * SEQ]
                    last = mm(dst, stack_k[0:SHIFT_ROW + 1, h, k * P:(k + 1) * P], stack_q[0:SHIFT_ROW + 1, h, :],
                              start=True, stop=(a == 1))
                    if a == 0:
                        for t in range(TT):
                            last = mm(dst[:, t * P:(t + 1) * P], bias_all[:, b * TT + t, k * P:(k + 1) * P], ident_bf[:, :],
                                      start=False, stop=(t == TT - 1))
                last.then_inc(s_sc, 1)

            def values(U, g):
                pe.wait_ge(s_exp, CREDIT + GH * (U + 1))
                pe.wait_ge(s_vones, U + 1)
                pe.wait_ge(s_oraw, U)
                for k in range(TT):
                    for i in range(GH):
                        last = mm(bank[4][32 * i:32 * i + 32, 0:SEQ], v_ones[:, k, GH * g + i, :],
                                  probs[:, g % 2, i, k * SEQ:(k + 1) * SEQ], start=(k == 0), stop=(k == TT - 1))
                last.then_inc(s_pv, 1)

            def turn_out(U):
                pe.wait_ge(s_oraw, U + 1)
                pe.wait_ge(s_on, U)
                for t in range(TT):
                    last = nc.tensor.transpose(bank[6][:, t * P:(t + 1) * P], o_raw[:, t * P:(t + 1) * P], ident[:, :])
                last.then_inc(s_ot, 1)

            def batch(b, last_batch, a):
                B = b + a * BATCH
                for g in range(GROUPS):
                    U = 4 * B + g
                    ahead = not (last_batch and g >= 2)
                    g2 = (g + 2) % GROUPS
                    b2 = b + 1 if g >= 2 else b
                    for i in range(GH):
                        scores(U, g, i, b, a)
                        if ahead:
                            max_scores(U + 2, g2, i, b2, a)
                    values(U, g)
                    if ahead:
                        turn_max(U + 2)
                    turn_out(U)
                pe.wait_ge(s_on, 4 * (B + 1))
                pe.wait_ge(s_end, B)
                turn(bank[7], o_norm).then_inc(s_t2, 1)
                pe.wait_ge(s_oT, B + 1)
                project(bank[7], 4 * a + 3, o_t).then_inc(s_wo, 1)

            for a in range(2):
                if a == 1:
                    pe.wait_ge(s_end, BATCH)
                with pe.Fori(0, BATCH // 2) as p:
                    projections(a, p)
                pe.wait_ge(s_v, BATCH * (a + 1))
                pe.wait_ge(s_hi["q"], BATCH * (a + 1))
                pe.wait_ge(s_hi["k"], BATCH * (a + 1))
                if a == 0:
                    pe.wait_ge(s_bias, BATCH)
                for g in range(2):
                    for i in range(GH):
                        max_scores(4 * a * BATCH + g, g, i, 0, a)
                    turn_max(4 * a * BATCH + g)
                with pe.Fori(0, BATCH - 1) as b:
                    batch(b, False, a)
                batch(BATCH - 1, True, a)

            pe.wait_ge(s_end, 2 * BATCH)
            pe.wait_ge(s_wts, 32)
            with pe.Fori(0, BATCH) as b:
                pe.wait_ge(s_x2s, b + 1)
                pe.wait_ge(s_fxT, b)
                turn(bank[0], x2s).then_inc(s_fx, 1)
                pe.wait_ge(s_fxT, b + 1)
                for e in range(EXPERTS):
                    n = b * EXPERTS + e
                    for m in range(MC):
                        if m >= 4:
                            pe.wait_ge(s_ha[m % 2], n * 4 + (m - 4) // 2 + 1)
                        else:
                            pe.wait_ge(s_ha[m % 2], n * 4)
                        for c in range(KC):
                            last = mm(bank[1 + m % 4][:, 0:SEQ], w1[:, e, c, m * P:(m + 1) * P], x2T[:, c, :],
                                      start=(c == 0), stop=(c == KC - 1))
                        last.then_inc(s_h, 1)
                    for j in range(2):
                        pe.wait_ge(s_ha[j], n * 4 + 4)
                    pe.wait_ge(s_yt, n)
                    for t in range(TT):
                        for m in range(MC):
                            last = mm(bank[5][:, t * E:(t + 1) * E], hidden[:, e % 2, m, t * P:(t + 1) * P], w2[:, e, m, :],
                                      start=(m == 0), stop=(m == MC - 1))
                    last.then_inc(s_y, 1)

        @block.scalar
        def _(act):
            act.wait_ge(s_const, 16 * 7)
            act.wait_ge(s_ident, 1)
            act.sem_inc(s_exp, CREDIT)
            act.sem_inc(s_pv, CREDIT)
            act.sem_inc(s_proj["v"], CREDIT)

            def projections(a, p):
                for s in range(2):
                    B = 2 * p + s + a * BATCH
                    act.wait_ge(s_tx, B + 1)
                    act.wait_ge(s_proj["v"], CREDIT + B - 1)
                    nc.scalar.activation(xT[:, s, :, :].rearrange("p t e -> p (t e)"), bank[s][:, :], ACT.Copy).then_inc(s_xT, 1)
                    if a == 0:
                        act.wait_ge(s_tc, B + 1)
                        nc.scalar.activation(cT[:, s, :, :].rearrange("p t e -> p (t e)"), bank[2 + s][:, :], ACT.Copy).then_inc(s_cT, 1)
                for s in range(2):
                    B = 2 * p + s + a * BATCH
                    for o in "qk":
                        act.wait_ge(s_proj[o], B + 1)
                        act.wait_ge(s_rest[o], B)
                        act.wait_ge(s_stored[o], 16 * B)
                        for t in range(KC):
                            bias = bias_qk[:, OPS[o], t:t + 1] if a else 0.0
                            if a and o == "q":
                                bias = bias_q_scaled[:, t:t + 1]
                            ps = bank[4 + OPS[o]][:, t * SEQ:(t + 1) * SEQ]
                            f = nc.scalar.activation(full[:, OPS[o], t, :], ps, ACT.Identity, bias=bias, scale=SCALE if o == "q" else 1.0)
                            hi = nc.scalar.activation(parts[:, OPS[o], 0, t, :], ps, ACT.Identity, bias=bias, scale=SCALE if o == "q" else 1.0)
                        f.then_inc(s_full[o], 1)
                        hi.then_inc(s_hi[o], 1)
                    for o in "qk":
                        act.wait_ge(s_rest[o], B + 1)
                        nc.scalar.activation(parts[:, OPS[o], 1, :, :], rest[:, OPS[o], :, :], ACT.Copy).then_inc(s_mid[o], 1)

            def batch(b, a):
                B = b + a * BATCH
                for g in range(GROUPS):
                    U = 4 * B + g
                    act.wait_ge(s_pv, CREDIT + U - 1)
                    for i in range(GH):
                        act.wait_ge(s_sc, GH * U + i + 1)
                        nc.scalar.activation(probs[:, g % 2, i, :], bank[2 + i % 2][:, :], ACT.Exp).then_inc(s_exp, 1)
                    act.wait_ge(s_pv, CREDIT + U + 1)
                    act.wait_ge(s_ot, U)
                    nc.scalar.activation(o_raw[:, :], bank[4][:, 0:SEQ], ACT.Copy).then_inc(s_oraw, 1)
                act.wait_ge(s_t2, B + 1)
                nc.scalar.activation(o_t[:, :, :].rearrange("p t e -> p (t e)"), bank[7][:, :], ACT.Copy).then_inc(s_oT, 1)

            for a in range(2):
                with act.Fori(0, BATCH // 2) as p:
                    projections(a, p)
                with act.Fori(0, BATCH) as b:
                    batch(b, a)

            with act.Fori(0, BATCH) as b:
                act.wait_ge(s_fx, b + 1)
                act.wait_ge(s_y, EXPERTS * b)
                nc.scalar.activation(x2T[:, :, :].rearrange("p t e -> p (t e)"), bank[0][:, :], ACT.Copy).then_inc(s_fxT, 1)
                for e in range(EXPERTS):
                    n = b * EXPERTS + e
                    for m in range(0, MC, 2):
                        act.wait_ge(s_h, n * MC + m + 1)
                        nc.scalar.activation(hidden[:, e % 2, m, :], bank[1 + m % 4][:, 0:SEQ], ACT.Relu,
                                             bias=b1_sb[:, e * MC + m:e * MC + m + 1]).then_inc(s_ha[0], 1)

        @block.gpsimd
        def _(pool):
            pool.memset(stack_k[SHIFT_ROW:SHIFT_ROW + 1, :, :], 1.0).then_inc(s_ones, 1)
            pool.wait_ge(s_ones, 1)
            pool.memset(v_ones[:, :, :, :], 1.0).then_inc(s_ones, 1)

            pool.memset(neg_half[:, :], -0.5).then_inc(s_ones, 1)

            def inverse_root(n):
                pool.wait_ge(s_vareps, n + 1)
                pool.wait_ge(s_ln, n)
                pool.tensor_tensor(rstd[:, :], var_eps[:, :], neg_half[:, :], ALU.pow).then_inc(s_rstd, 1)

            def split(B):
                for o in "qk":
                    n = OPS[o]
                    pool.wait_ge(s_full[o], B + 1)
                    pool.wait_ge(s_hi[o], B + 1)
                    pool.wait_ge(s_lo[o], B)
                    pool.tensor_tensor(rest[:, n, :, :], full[:, n, :, :], parts[:, n, 0, :, :], ALU.subtract).then_inc(s_rest[o], 1)
                for o in "qk":
                    n = OPS[o]
                    pool.wait_ge(s_mid[o], B + 1)
                    pool.tensor_tensor(parts[:, n, 2, :, :], rest[:, n, :, :], parts[:, n, 1, :, :], ALU.subtract).then_inc(s_lo[o], 1)

            def spread_v(b, g):
                hs = slice(GH * HD * g, GH * HD * (g + 1))
                pool.tensor_copy(v_ones[:, :, GH * g:GH * g + GH, 0:HD],
                                 v_all[:, tiles(b), hs].rearrange("p t (h d) -> p t h d", h=GH)).then_inc(s_vones, 1)

            pool.wait_ge(s_const, 16 * 7)
            pool.wait_ge(s_ones, 3)
            for a in range(2):
                with pool.Fori(0, BATCH // 2) as p:
                    if a == 0:
                        for s in range(2):
                            inverse_root(2 * p + s)
                    for s in range(2):
                        split(2 * p + s + a * BATCH)
                pool.wait_ge(s_v, BATCH * (a + 1))
                for g in range(GROUPS):
                    if a == 1:
                        pool.wait_ge(s_pv, CREDIT + 4 * BATCH)
                    spread_v(0, g)

                def batch(b, last):
                    B = b + a * BATCH
                    pool.wait_ge(s_end, B)
                    if a == 0:
                        pool.wait_ge(s_xres, 16 * (b + 1))
                        pool.wait_ge(s_x1st, 16 * b)
                        for t in range(TT):
                            r = pool.tensor_tensor(resid[:, t, :], xres[:, t, :], V["bo0"], ALU.add)
                    else:
                        for t in range(TT):
                            r = pool.tensor_tensor(resid[:, t, :], src_all[:, b * TT + t, :], V["bo1"], ALU.add)
                    r.then_inc(s_res, 1)
                    if not last:
                        for g in range(GROUPS):
                            pool.wait_ge(s_pv, CREDIT + 4 * B + g + 1)
                            spread_v(b + 1, g)
                    inverse_root(BATCH + B)

                if a == 1:
                    pool.wait_ge(s_x1st, 16 * BATCH)
                with pool.Fori(0, BATCH - 1) as b:
                    batch(b, False)
                batch(BATCH - 1, True)

            with pool.Fori(0, BATCH) as b:
                inverse_root(3 * BATCH + b)

        @block.vector
        def _(dve):
            step = [0]

            def link(ins):
                step[0] += 1
                ins.then_inc(s_step, 1)
                dve.wait_ge(s_step, step[0])

            dve.wait_ge(s_const, 16 * 7)
            link(nc.vector.tensor_copy(ident_bf[:, :], ident[:, :]))
            nc.vector.tensor_scalar(bias_q_scaled[:, :], bias_qk[:, 0, :], SCALE, None, ALU.mult).then_inc(s_ident, 1)

            def layer_norm(n, src, dst):
                for t in range(TT):
                    i = nc.vector.bn_stats(stats[:, t, :], src(t))
                i.then_inc(s_stats, 1)
                dve.wait_ge(s_stats, n + 1)
                dve.sem_inc(s_gate, 1)
                for t in range(TT):
                    i = nc.vector.bn_aggr(mv[:, t, :], stats[:, t, :])
                i.then_inc(s_aggr, 1)
                dve.wait_ge(s_aggr, n + 1)
                nc.vector.tensor_scalar(var_eps[:, :], mv[:, :, 1], EPS, None, ALU.add).then_inc(s_vareps, 1)
                dve.wait_ge(s_rstd, n + 1)
                for t in range(TT):
                    i = nc.vector.tensor_scalar(dst(t), src(t), mv[:, t, 0:1], rstd[:, t:t + 1], ALU.subtract, ALU.mult)
                i.then_inc(s_ln, 1)

            def take_v(a, b):
                B = b + a * BATCH
                dve.wait_ge(s_proj["v"], CREDIT + B + 1)
                for t in range(TT):
                    ps = bank[6][:, t * E:(t + 1) * E]
                    if a:
                        i = nc.vector.tensor_tensor(v_all[:, b * TT + t, :], ps, V["bv1"], ALU.add)
                    else:
                        i = nc.vector.tensor_copy(v_all[:, b * TT + t, :], ps)
                i.then_inc(s_v, 1)

            def projections0(p):
                for s in range(2):
                    b = 2 * p + s
                    dve.wait_ge(s_xin[s], 16 * p + 16)
                    layer_norm(b, lambda t: xb[:, s, t, :], lambda t: xb[:, s, t, :])
                for s in range(2):
                    b = 2 * p + s
                    dve.wait_ge(s_min[s], 16 * p + 16)
                    nc.vector.tensor_reduce(seen[:, tiles(b)], mask_u8[:, s, :, :], AX.X, ALU.max)
                    nc.vector.tensor_scalar(bias_all[:, tiles(b), :], mask_u8[:, s, :, :], MASKED, -MASKED, ALU.mult, ALU.add).then_inc(s_bias, 1)
                    take_v(0, b)

            with dve.Fori(0, BATCH // 2) as p:
                projections0(p)
            dve.wait_ge(s_bias, BATCH)
            link(nc.vector.tensor_tensor(seen[:, :], seen[:, :], pad_sb[:, :], ALU.mult))
            link(nc.vector.reciprocal(nan_all[:, :], seen[:, :]))
            link(nc.vector.tensor_scalar(nan_all[:, :], nan_all[:, :], 0.0, None, ALU.mult))

            def max_head(U, i):
                n = GH * U + i
                dve.wait_ge(s_mm, n + 1)
                if i == 0:
                    dve.wait_ge(s_nt, U)
                nc.vector.tensor_reduce(negmax[:, TT * i:TT * i + TT], bank[i % 2][:, :].rearrange("p (t k) -> p t k", t=TT),
                                        AX.X, ALU.max, negate=True).then_inc(s_max, 1)

            def max_unit(U):
                for i in range(GH):
                    max_head(U, i)

            def copy_max(U):
                dve.wait_ge(s_nt, U + 1)
                dve.wait_ge(s_row, 16 * U)
                nc.vector.tensor_copy(negmax_t[:, :], bank[5][0:GH * TT, 0:P // 2].bitcast(BF16)).then_inc(s_ntc, 1)

            def normalise(U, g, B):
                dve.wait_ge(s_ot, U + 1)
                o4 = bank[6][:, 0:TT * P].rearrange("p (t h d) -> p t h d", t=TT, h=GH)
                nc.vector.reciprocal(rden[:, :, :], o4[:, :, :, HD]).then_inc(s_rden, 1)
                dve.wait_ge(s_rden, U + 1)
                if g == 0:
                    dve.wait_ge(s_t2, B)
                for t in range(TT):
                    i = nc.vector.tensor_tensor(o_norm[:, t, GH * HD * g:GH * HD * (g + 1)].rearrange("p (h d) -> p h d", h=GH),
                                                o4[:, t, :, 0:HD], rden[:, t, :].unsqueeze(2).broadcast_to([P, GH, HD]), ALU.mult)
                i.then_inc(s_on, 1)

            def batch(b, last, a):
                B = b + a * BATCH
                for g in range(GROUPS):
                    U = 4 * B + g
                    if not (last and g >= 2):
                        max_unit(U + 2)
                        copy_max(U + 2)
                    normalise(U, g, B)
                dve.wait_ge(s_wo, B + 1)
                dve.wait_ge(s_res, B + 1)
                for t in range(TT):
                    ps = bank[7][:, t * E:(t + 1) * E]
                    if a == 0:
                        i = nc.vector.scalar_tensor_tensor(resid[:, t, :], ps, nan_all[:, bass.ds(b * TT + t, 1) if not isinstance(b, int) else slice(b * TT + t, b * TT + t + 1)],
                                                           resid[:, t, :], ALU.add, ALU.add)
                    else:
                        i = nc.vector.tensor_tensor(resid[:, t, :], ps, resid[:, t, :], ALU.add)
                i.then_inc(s_x1, 1)
                dve.wait_ge(s_x1, B + 1)
                dst = (lambda t: x2s[:, t, :]) if a else (lambda t: src_all[:, b * TT + t, :])
                layer_norm(BATCH + B, lambda t: resid[:, t, :], dst)
                if a == 1:
                    dve.wait_ge(s_ln, BATCH + B + 1)
                    for t in range(TT):
                        x = x2s[:, t, :]
                        i = nc.vector.tensor_tensor(x, x, V["ln1g"], ALU.mult)
                    i.then_inc(s_y1, 1)
                    dve.wait_ge(s_y1, b + 1)
                    for t in range(TT):
                        x = x2s[:, t, :]
                        i = nc.vector.tensor_tensor(x, x, V["ln1b"], ALU.add)
                    i.then_inc(s_y2, 1)
                    dve.wait_ge(s_y2, b + 1)
                    nc.vector.tensor_copy(src_all[:, tiles(b), :], x2s[:, :, :])
                    for t in range(TT):
                        i = nc.vector.tensor_tensor_reduce(resid[:, t, :], x2s[:, t, :], V["rw"], 1.0, 0.0,
                                                           ALU.mult, ALU.add, keys_b[:, t:t + 1])
                    i.then_inc(s_keys, 1)
                    dve.wait_ge(s_keys, b + 1)
                    nc.vector.tensor_copy(keys[:, tiles(b)], keys_b[:, :]).then_inc(s_end, 1)
                else:
                    dve.wait_ge(s_ln, BATCH + B + 1)
                    nc.vector.tensor_copy(keys_b[:, :], rstd[:, :]).then_inc(s_end, 1)

            for a in range(2):
                if a == 1:
                    with dve.Fori(0, BATCH // 2) as p:
                        for s in range(2):
                            b = 2 * p + s
                            dve.wait_ge(s_tx, BATCH + b - 1)
                            nc.vector.tensor_copy(xb[:, s, :, :], src_all[:, tiles(b), :]).then_inc(s_src, 1)
                        for s in range(2):
                            take_v(1, 2 * p + s)
                for g in range(2):
                    max_unit(4 * a * BATCH + g)
                    copy_max(4 * a * BATCH + g)
                with dve.Fori(0, BATCH - 1) as b:
                    batch(b, False, a)
                batch(BATCH - 1, True, a)

            def floor(dst, src, tmp):
                link(nc.vector.tensor_copy(route_i[:, :], src))
                link(nc.vector.tensor_copy(dst, route_i[:, :]))
                link(nc.vector.tensor_tensor(tmp, dst, src, ALU.is_gt))
                link(nc.vector.tensor_tensor(dst, dst, tmp, ALU.subtract))

            R = [route[:, i, :] for i in range(6)]
            dve.wait_ge(s_end, 2 * BATCH)
            link(nc.vector.tensor_scalar(R[0], keys[:, :], rb_sb[:, 0:1], None, ALU.add))
            floor(R[1], R[0], R[2])
            link(nc.vector.tensor_scalar(R[3], R[1], 1.0 / EXPERTS, None, ALU.mult))
            floor(R[4], R[3], R[2])
            link(nc.vector.tensor_scalar(R[4], R[4], -float(EXPERTS), None, ALU.mult))
            link(nc.vector.tensor_tensor(R[5], R[1], R[4], ALU.add))
            for e in range(EXPERTS):
                link(nc.vector.tensor_scalar(onehot[:, e, :], R[5], float(e), None, ALU.is_equal))

            with dve.Fori(0, BATCH) as b:
                dve.wait_ge(s_fx, b)
                nc.vector.tensor_copy(x2s[:, :, :], src_all[:, tiles(b), :]).then_inc(s_x2s, 1)
                for e in range(EXPERTS):
                    n = b * EXPERTS + e
                    for m in range(1, MC, 2):
                        dve.wait_ge(s_h, n * MC + m + 1)
                        nc.vector.tensor_scalar(hidden[:, e % 2, m, :], bank[1 + m % 4][:, 0:SEQ],
                                                b1_sb[:, e * MC + m:e * MC + m + 1], 0.0, ALU.add, ALU.max).then_inc(s_ha[1], 1)
                    dve.wait_ge(s_y, n + 1)
                    if e == 0:
                        dve.wait_ge(s_out, 16 * b)
                    for t in range(TT):
                        i = nc.vector.tensor_tensor(resid[:, t, :], bank[5][:, t * E:(t + 1) * E], V[f"b2_{e}"], ALU.add)
                    i.then_inc(s_yt, 1)
                    dve.wait_ge(s_yt, n + 1)
                    for t in range(TT):
                        acc = src_all[:, b * TT + t, :]
                        oh = onehot[:, e, bass.ds(b * TT + t, 1)]
                        i = nc.vector.scalar_tensor_tensor(ff[:, t, :], resid[:, t, :], oh, acc if e == 0 else ff[:, t, :], ALU.mult, ALU.add)
                    i.then_inc(s_step2, 1)
                    dve.wait_ge(s_step2, n + 1)
                layer_norm(3 * BATCH + b, lambda t: ff[:, t, :], lambda t: resid[:, t, :])
                dve.wait_ge(s_ln, 3 * BATCH + b + 1)
                for t in range(TT):
                    i = nc.vector.tensor_tensor(resid[:, t, :], resid[:, t, :], V["ln2g"], ALU.mult)
                i.then_inc(s_f1, 1)
                dve.wait_ge(s_f1, b + 1)
                for t in range(TT):
                    i = nc.vector.tensor_tensor(resid[:, t, :], resid[:, t, :], V["ln2b"], ALU.add)
                i.then_inc(s_f2, 1)
                dve.wait_ge(s_f2, b + 1)
                dve.wait_ge(s_x1in, 16 * (b + 1))
                for t in range(TT):
                    i = nc.vector.tensor_tensor(resid[:, t, :], resid[:, t, :], xres[:, t, :], ALU.add)
                i.then_inc(s_outr, 1)


def kernel(**inputs):
    import concourse.bacc as bacc
    from concourse.bass_utils import run_bass_kernel_spmd

    I = {k: np.asarray(v) for k, v in inputs.items()}
    x0, f = "L0_xattn_", "L0_ffn_"

    def by_dim(w):
        return w.reshape(E, HEADS, HD).transpose(0, 2, 1).reshape(E, E)

    w_attn = np.stack([
        by_dim(I[x0 + "Wq"].T), by_dim(I[x0 + "Wk"].T), I[x0 + "Wv"].T, I[x0 + "Wo"].T,
        by_dim(I[f + "Wq"]), by_dim(I[f + "Wk"]), I[f + "Wv"], I[f + "Wo"],
    ])
    vec = np.stack([
        I[x0 + "bo"], I[f + "bv"], I[f + "bo"], I[f + "ln1_g"], I[f + "ln1_b"], I[f + "ln2_g"], I[f + "ln2_b"],
        I[f + "router_w"][:, 0], *I[f + "b2"],
    ])
    bias_qk = np.stack([I[f + n].reshape(HEADS, HD).T.reshape(KC, P) for n in ("bq", "bk")])
    arrays = {
        "x": I["x"].reshape(BATCH * SEQ, E),
        "ctx": I["ctx_1024"].reshape(BATCH * SEQ, E),
        "mask": I["mask_BxSxS2_bf1"].reshape(BATCH * SEQ, SEQ).view(np.uint8),
        "pad": I["mask_BxS2_bf1"].view(np.uint8).reshape(BATCH * TT, P).T,
        "w_attn": w_attn,
        "vec": vec,
        "bias_qk": bias_qk.transpose(2, 0, 1),
        "b1": I[f + "b1"].reshape(EXPERTS * MC, P).T,
        "rb": I[f + "router_b"],
        "w1": I[f + "W1"],
        "w2": I[f + "W2"],
        "ident": np.eye(P, dtype=np.float32),
    }
    nc = bacc.Bacc("TRN2", target_bir_lowering=False, num_devices=1)
    io, given = {}, {}
    for name, a in arrays.items():
        a = np.ascontiguousarray(a)
        given[f"in_{name}"] = a
        io[name] = nc.dram_tensor(f"in_{name}", a.shape, mybir.dt.from_np(a.dtype), kind="ExternalInput").ap()
    io["out"] = nc.dram_tensor("out_x", (BATCH * SEQ, E), F32, kind="ExternalOutput").ap()
    build(nc, io)
    r = run_bass_kernel_spmd(nc, [given], core_ids=[0])
    return r.results[0]["out_x"].reshape(BATCH, SEQ, E)
```

```python
import numpy as np
import concourse.bass as bass
from concourse import mybir
from contextlib import ExitStack

F32 = mybir.dt.float32
BF16 = mybir.dt.bfloat16
U8 = mybir.dt.uint8
I32 = mybir.dt.int32
ALU = mybir.AluOpType
ACT = mybir.ActivationFunctionType
AX = mybir.AxisListType

P = 128
BATCH, SEQ, E = 8, 256, 256
HEADS, HD = 16, 16
DFF, EXPERTS = 1024, 4
TT = SEQ // P
KC = E // P
GROUPS, GH = 4, 4
TERMS = 6
SHIFT_ROW = TERMS * HD
Q_LOADS = ((0, 0, 3), (3, 1, 2), (5, 2, 1))
K_LOADS = ((0, 0, 3), (3, 0, 2), (5, 0, 1))
STACK_LOADS = len(Q_LOADS) + len(K_LOADS)
HALF = HEADS // 2
SCALE = float(HD) ** -0.5
EPS = 1e-5
MASKED = 1e30
CREDIT = 2
ONE = 1
N_CONST = 8
MC = DFF // P
TILES = BATCH * TT
SORTED = (BATCH * SEQ + EXPERTS * (P - 1)) // P
VECS = ("bo0", "bv1", "bo1", "ln1g", "ln1b", "ln2g", "ln2b", "rw", "b2_0", "b2_1", "b2_2", "b2_3")


def build(nc, io):
    ctx = ExitStack()
    with ctx:
        def sb(name, shape, dt=F32):
            return ctx.enter_context(nc.sbuf_tensor(name, shape, dt))

        def sem(name):
            return ctx.enter_context(nc.semaphore(name))

        def dram(name, shape, dt):
            return nc.dram_tensor(name, shape, dt, kind="Internal").ap()

        w_attn = sb("w_attn", [P, 8, KC, E])
        vec = sb("vec", [P, len(VECS), E])
        ident = sb("ident", [P, P])
        ident_bf = sb("ident_bf", [P, P], BF16)
        bias_qk = sb("bias_qk", [P, 2, KC])
        tri_ones = sb("tri_ones", [P, 2, P])
        rb_sb = sb("rb_sb", [P, 1])
        pad_sb = sb("pad_sb", [P, BATCH * TT], U8)
        w1 = sb("w1", [P, EXPERTS, KC, DFF])
        w2 = sb("w2", [P, EXPERTS, MC, E])
        flat = w1[:, :, :, :].rearrange("p a b c -> p (a b c)")
        SLOT = TT * E

        def view(n, slots):
            return flat[:, n * SLOT:(n + slots) * SLOT]

        xb = view(0, 2).rearrange("p (s t e) -> p s t e", s=2, t=TT)
        cb = view(2, 2).rearrange("p (s t e) -> p s t e", s=2, t=TT)
        xT = view(4, 2).rearrange("p (s t e) -> p s t e", s=2, t=KC)
        cT = view(6, 2).rearrange("p (s t e) -> p s t e", s=2, t=KC)
        full = view(8, 2).rearrange("p (s t e) -> p s t e", s=2, t=KC)
        rest = view(10, 2).rearrange("p (s t e) -> p s t e", s=2, t=KC)
        parts = view(12, 3).bitcast(BF16).rearrange("p (o r t e) -> p o r t e", o=2, r=3, t=KC)
        mask_u8 = sb("mask_u8", [P, 2, TT, SEQ], U8)

        src_all = sb("src_all", [P, BATCH * TT, E])
        v_all = sb("v_all", [P, BATCH * TT, E])
        bias_all = sb("bias_all", [P, BATCH * TT, SEQ], BF16)
        seen = sb("seen", [P, BATCH * TT])
        nan_all = sb("nan_all", [P, BATCH * TT])
        stack_q = sb("stack_q", [P, 2, HEADS, SEQ], BF16)
        stack_k = sb("stack_k", [P, 2, HEADS, SEQ], BF16)
        probs = sb("probs", [P, 2, GH, TT * SEQ])
        v_ones = sb("v_ones", [P, TT, HEADS, 2 * HD])
        negmax = sb("negmax", [P, GH * TT], BF16)
        negmax_t = sb("negmax_t", [GH * TT, P], BF16)
        o_raw = sb("o_raw", [P, SEQ])
        rden = sb("rden", [P, TT, GH])
        o_norm = sb("o_norm", [P, TT, E])
        o_t = sb("o_t", [P, KC, SEQ])
        xres = sb("xres", [P, TT, E])
        resid = sb("resid", [P, TT, E])
        stats = sb("stats", [P, TT, 6])
        mv = sb("mv", [P, TT, 2])
        rstd = sb("rstd", [P, TT])
        var_eps = sb("var_eps", [P, TT])
        neg_half = sb("neg_half", [P, TT])
        keys_b = sb("keys_b", [P, TT])
        keys = sb("keys", [P, BATCH * TT])
        route = sb("route", [P, 6, TILES])
        route_i = sb("route_i", [P, TILES], I32)
        onehot = sb("onehot", [P, EXPERTS, TILES])
        count_a = sb("count_a", [P, EXPERTS, TILES])
        count_b = sb("count_b", [P, EXPERTS, TILES])
        small = sb("small", [P, 6, EXPERTS])
        small_i = sb("small_i", [P, EXPERTS], I32)
        tile_no = sb("tile_no", [P, SORTED])
        tile_e = sb("tile_e", [P, 2, SORTED])
        expert_of = sb("expert_of", [P, SORTED], I32)
        place = sb("place", [P, TILES], I32)
        bias_q_scaled = sb("bias_q_scaled", [P, KC])
        x2s = sb("x2s", [P, TT, E])
        b1_sb = v_all[:, :, :].rearrange("p t e -> p (t e)").rearrange("p (n f) -> p n f", n=EXPERTS)
        x1_all = probs[:, :, :, :].rearrange("p s h (b e) -> p (s h b) e", e=E)
        hid = stack_q[:, 0, :, :].bitcast(F32).rearrange("p h s -> p (h s)")[:, 0:DFF]
        hid_t = stack_k[:, 0, :, :].bitcast(F32).rearrange("p h s -> p (h s)")[:, 0:DFF].rearrange("p (m t) -> p m t", m=MC)
        xg = xres[:, 0, :]
        xr = xres[:, 1, :]
        xg_t = o_t[:, 0, :].rearrange("p (c t) -> p c t", c=KC)
        z_a, z_b = resid[:, 0, :], resid[:, 1, :]
        z_out = o_norm[:, 0, :]

        bank = [ctx.enter_context(nc.psum_tensor(f"bank{i}", [P, 512], F32)) for i in range(8)]

        q_dram = dram("q_parts", [2 * BATCH, 3, HD, HEADS, SEQ], BF16)
        k_dram = dram("k_parts", [2 * BATCH, 3, HD, HEADS, SEQ], BF16)
        x1_dram = dram("x1_keep", [BATCH * SEQ, E], F32)
        sorted_x = dram("sorted_x", [SORTED * P, E], F32)
        sorted_z = dram("sorted_z", [SORTED * P, E], F32)

        s_const = sem("constants_loaded")
        s_ident = sem("ident_bf_ready")
        s_ones = sem("ones_ready")
        s_wts = sem("ffn_weights_loaded")
        s_xin = [sem(f"x_loaded{s}") for s in range(2)]
        s_cin = [sem(f"ctx_loaded{s}") for s in range(2)]
        s_min = [sem(f"mask_loaded{s}") for s in range(2)]
        s_bias = sem("mask_bias_ready")
        s_nan = sem("nan_ready")
        s_stats, s_aggr, s_rstd, s_ln = sem("stats_done"), sem("aggr_done"), sem("rstd_done"), sem("ln_done")
        s_tx, s_tc = sem("x_transposed"), sem("ctx_transposed")
        s_xT, s_cT = sem("xT_ready"), sem("cT_ready")
        s_proj = {o: sem(f"{o}_projected") for o in "qkv"}
        s_full = {o: sem(f"{o}_full_ready") for o in "qk"}
        s_hi = {o: sem(f"{o}_hi_ready") for o in "qk"}
        s_rest = {o: sem(f"{o}_rest_ready") for o in "qk"}
        s_mid = {o: sem(f"{o}_mid_ready") for o in "qk"}
        s_lo = {o: sem(f"{o}_lo_ready") for o in "qk"}
        s_stored = {o: sem(f"{o}_parts_stored") for o in "qk"}
        s_v = sem("v_ready")
        s_stack = [[sem(f"stack_loaded{s}{h}") for h in range(2)] for s in range(2)]
        s_row = sem("shift_row_loaded")
        s_vones = sem("v_ones_ready")
        s_mm = sem("max_scores_ready")
        s_max = sem("max_taken")
        s_nt = sem("negmax_transposed")
        s_ntc = sem("negmax_t_ready")
        s_sc = sem("scores_ready")
        s_exp = sem("probs_ready")
        s_pv = sem("pv_done")
        s_oraw = sem("o_raw_ready")
        s_ot = sem("o_raw_transposed")
        s_rden = sem("rden_ready")
        s_on = sem("o_norm_ready")
        s_t2 = sem("o_norm_transposed")
        s_oT = sem("o_t_ready")
        s_wo = sem("out_projected")
        s_xres = sem("xres_loaded")
        s_res = sem("resid_ready")
        s_x1 = sem("x1_ready")
        s_x1st = sem("x1_stored")
        s_end = sem("attention_batch_done")
        s_vareps = sem("var_eps_ready")
        s_gate = sem("stats_gate")
        s_step = sem("vector_step")
        s_keys = sem("router_keys_ready")
        s_zero, s_filled = sem("zeros_ready"), sem("sorted_x_cleared")
        s_oh, s_rank = sem("onehot_ready"), sem("ranks_ready")
        s_place, s_eof = sem("places_ready"), sem("tile_experts_ready")
        s_scat = sem("x2_scattered")
        s_b1in = sem("b1_loaded")
        s_xg, s_xr = sem("sorted_x_loaded"), sem("sorted_residual_loaded")
        s_gx, s_gxT = sem("sorted_x_transposed"), sem("sorted_xT_ready")
        s_h = sem("hidden_psum_ready")
        s_hb = sem("hidden_biased")
        s_ht = sem("hidden_transposed")
        s_hT = sem("hidden_t_ready")
        s_y = sem("expert_out_ready")
        s_yb = sem("expert_out_biased")
        s_yr = sem("ffn_residual_added")
        s_z, s_zst = sem("z_ready"), sem("z_stored")
        s_gath = [sem(f"z_gathered{t}") for t in range(TILES)]
        s_x1in = sem("x1_loaded")
        s_outr = sem("out_ready")
        s_src = sem("src_staged")
        s_y1, s_y2 = sem("ln1_scaled"), sem("x2_ready")
        s_f1 = sem("ln2_scaled")
        s_out = sem("out_stored")

        x_d, c_d, m_d, out_d = io["x"], io["ctx"], io["mask"], io["out"]
        OPS = {"q": 0, "k": 1}
        V = {n: vec[:, i, :] for i, n in enumerate(VECS)}
        block = ctx.enter_context(nc.Block())

        def tiles(b):
            return slice(b * TT, b * TT + TT) if isinstance(b, int) else bass.ds(b * TT, TT)

        def rows(b):
            return slice(b * SEQ, b * SEQ + SEQ) if isinstance(b, int) else bass.ds(b * SEQ, SEQ)

        def each_unit(eng, unit):
            for g in range(3):
                unit(0, g, 0, 0, True, True)
            with eng.Fori(0, BATCH // 2 - 1) as r:
                for s in range(2):
                    b = 2 * r + s
                    unit(b, 3, s, r, False, True)
                    for g in range(3):
                        unit(b + 1, g, 1 - s, r + s, False, True)
            b = BATCH - 2
            unit(b, 3, 0, b // 2, False, True)
            for g in range(GROUPS):
                unit(b + 1, g, 1, b // 2, False, g < 2)

        def two_ahead(b, g, s, r):
            return (b, g + 2, s, r) if g < 2 else (b + 1, g - 2, 1 - s, r + s)

        @block.sync
        def _(sp):
            sp.sem_inc(s_row, ONE)
            sp.sem_inc(s_x1st, ONE)
            sp.sem_inc(s_zst, ONE)
            sp.sem_inc(s_filled, ONE)
            sp.sem_inc(s_stored["q"], ONE)
            sp.sem_inc(s_stored["k"], ONE)
            sp.dma_start(w_attn[:, :, :, :], io["w_attn"].rearrange("n (c p) e -> p n c e", p=P)).then_inc(s_const, 16)
            sp.dma_start(ident[:, :], io["ident"]).then_inc(s_const, 16)
            sp.dma_start(vec[:, :, :], io["vec"].partition_broadcast(P)).then_inc(s_const, 16)
            sp.dma_start(bias_qk[:, :, :], io["bias_qk"]).then_inc(s_const, 16)
            sp.dma_start(tri_ones[:, :, :], io["tri_ones"]).then_inc(s_const, 16)
            sp.dma_start(tile_no[:, :], io["tile_no"].partition_broadcast(P)).then_inc(s_const, 16)
            sp.dma_start(rb_sb[:, :], io["rb"].partition_broadcast(P)).then_inc(s_const, 16)
            sp.dma_start(pad_sb[:, :], io["pad"]).then_inc(s_const, 16)

            def load_inputs(b, s):
                sp.dma_start(xb[:, s, :, :], x_d[rows(b), :].rearrange("(t p) e -> p t e", p=P)).then_inc(s_xin[s], 16)
                sp.dma_start(cb[:, s, :, :], c_d[rows(b), :].rearrange("(t p) e -> p t e", p=P)).then_inc(s_cin[s], 16)
                sp.dma_start(mask_u8[:, s, :, :], m_d[rows(b), :].rearrange("(t p) e -> p t e", p=P)).then_inc(s_min[s], 16)

            def store_parts(B):
                for o in "qk":
                    sp.wait_ge(s_mid[o], ONE + B + 1)
                    sp.wait_ge(s_lo[o], ONE + B + 1)
                    dst = (q_dram if o == "q" else k_dram)[B]
                    sp.dma_start(dst.rearrange("r (t d) h k -> (d h) r t k", t=KC), parts[:, OPS[o], :, :, :]).then_inc(s_stored[o], 16)

            def load_stack(B, s, half):
                hs = slice(HALF * half, HALF * half + HALF)
                for r, part, n in Q_LOADS:
                    sp.dma_start(stack_q[HD * r:HD * (r + n), s, hs, :],
                                 q_dram[B, part:part + 1, :, hs, :].to_broadcast([n, HD, HALF, SEQ])).then_inc(s_stack[s][half], 16)
                for r, p0, n in K_LOADS:
                    sp.dma_start(stack_k[HD * r:HD * (r + n), s, hs, :],
                                 k_dram[B, p0:p0 + n, :, hs, :].rearrange("r d h k -> (r d) h k")).then_inc(s_stack[s][half], 16)

            def shift_row(U, g, s):
                sp.wait_ge(s_ntc, ONE + U + 1)
                sp.dma_start(stack_q[SHIFT_ROW:SHIFT_ROW + 1, s, GH * g:GH * g + GH, :].rearrange("o h (t k) -> o (h t) k", t=TT),
                             negmax_t[:, :]).then_inc(s_row, 16)

            def load_xres(b):
                sp.dma_start(xres[:, :, :], x_d[rows(b), :].rearrange("(t p) e -> p t e", p=P)).then_inc(s_xres, 16)

            for s in range(2):
                load_inputs(s, s)
            sp.wait_ge(s_zero, 1)
            with sp.Fori(0, SORTED) as j:
                sp.dma_start(sorted_x[bass.ds(j * P, P), :], x2s[:, 0, :]).then_inc(s_filled, 16)
            with sp.Fori(0, BATCH // 2 - 1) as p:
                for s in range(2):
                    b = 2 * p + s
                    store_parts(b)
                    sp.wait_ge(s_tx, b + 1)
                    sp.wait_ge(s_tc, b + 1)
                    sp.wait_ge(s_bias, b + 1)
                    load_inputs(b + 2, s)
            for b in (BATCH - 2, BATCH - 1):
                store_parts(b)

            for a in range(2):
                if a == 1:
                    with sp.Fori(0, BATCH) as b:
                        store_parts(b + BATCH)
                    for o in "qk":
                        sp.wait_ge(s_stored[o], ONE + 16 * 2 * BATCH)
                    sp.wait_ge(s_proj["v"], CREDIT + 2 * BATCH)
                    sp.dma_start(w1[:, :, :, :], io["w1"].rearrange("n (c p) f -> p n c f", p=P)).then_inc(s_wts, 16)
                    sp.dma_start(w2[:, :, :, :], io["w2"].rearrange("n (c p) e -> p n c e", p=P)).then_inc(s_wts, 16)
                B0 = a * BATCH
                for o in "qk":
                    sp.wait_ge(s_stored[o], ONE + 16 * (B0 + 2))
                for s in range(2):
                    for half in range(2):
                        load_stack(B0 + s, s, half)
                if a == 0:
                    load_xres(0)
                for g in range(2):
                    shift_row(4 * B0 + g, g, 0)

                def unit(b, g, s, r, first, ahead):
                    B = b + B0
                    U = 4 * B + g
                    if ahead:
                        _, g2, s2, _ = two_ahead(b, g, s, r)
                        shift_row(U + 2, g2, s2)
                    if g == 3 and not isinstance(b, int):
                        for o in "qk":
                            sp.wait_ge(s_stored[o], ONE + 16 * (B + 3))
                        load_stack(B + 2, s, 0)
                    if g == 0 and not isinstance(b, int):
                        load_stack(B + 1, 1 - s, 1)
                    if a == 0 and g == 3 and not (isinstance(b, int) and b == BATCH - 1):
                        sp.wait_ge(s_res, B + 1)
                        load_xres(b + 1)
                    if a == 0 and g == 2 and not first:
                        store_x1(b - 1)

                def store_x1(b):
                    sp.wait_ge(s_x1, b + 1)
                    sp.dma_start(x1_dram[rows(b), :].rearrange("(t p) e -> p t e", p=P), resid[:, :, :]).then_inc(s_x1st, 16)

                each_unit(sp, unit)
                if a == 0:
                    store_x1(BATCH - 1)

            sp.wait_ge(s_vones, 4 * 2 * BATCH)
            sp.dma_start(b1_sb, io["b1"].partition_broadcast(P)).then_inc(s_b1in, 16)
            sp.wait_ge(s_x1st, ONE + 16 * BATCH)
            sp.wait_ge(s_pv, CREDIT + 4 * 2 * BATCH)
            sp.dma_start(x1_all, x1_dram.rearrange("(t p) e -> p t e", p=P)).then_inc(s_x1in, 16)

            sp.wait_ge(s_end, ONE + 2 * BATCH)
            sp.wait_ge(s_filled, ONE + 16 * SORTED)
            sp.wait_ge(s_scat, 16 * TILES)

            def load_x(row):
                sp.dma_start(xg, sorted_x[bass.ds(row, P), :]).then_inc(s_xg, 16)

            def load_residual(row):
                sp.dma_start(xr, sorted_x[bass.ds(row, P), :]).then_inc(s_xr, 16)

            def store_z(j, row):
                sp.wait_ge(s_z, j + 1)
                sp.dma_start(sorted_z[bass.ds(row, P), :], z_out).then_inc(s_zst, 16)

            load_x(0)
            load_residual(0)
            sp.wait_ge(s_gx, 1)
            load_x(P)
            with sp.Fori(1, SORTED - 1) as j:
                row, before, after = sp.snap(j * P), sp.snap(j * P - P), sp.snap(j * P + P)
                sp.wait_ge(s_gx, j + 1)
                load_x(after)
                sp.wait_ge(s_yr, j)
                load_residual(row)
                store_z(j - 1, before)
            sp.wait_ge(s_yr, SORTED - 1)
            load_residual((SORTED - 1) * P)
            for j in (SORTED - 2, SORTED - 1):
                store_z(j, j * P)

            for t in range(TILES):
                sp.wait_ge(s_outr, t + 1)
                sp.dma_start(out_d[t * P:(t + 1) * P, :], src_all[:, t, :]).then_inc(s_out, 16)
            sp.wait_ge(s_out, 16 * TILES)

        @block.tensor
        def _(pe):
            pe.sem_inc(s_nt, ONE)
            pe.sem_inc(s_ot, ONE)
            pe.sem_inc(s_t2, ONE)
            mm = nc.tensor.matmul
            pe.wait_ge(s_const, 16 * N_CONST)
            pe.wait_ge(s_ident, 1)

            def turn(dst, src):
                for c in range(KC):
                    for t in range(TT):
                        last = nc.tensor.transpose(dst[:, c * SEQ + t * P:c * SEQ + (t + 1) * P], src[:, t, c * P:(c + 1) * P], ident[:, :])
                return last

            def project_t(dst, w, xt):
                for t in range(KC):
                    for c in range(KC):
                        last = mm(dst[:, t * SEQ:(t + 1) * SEQ], w_attn[:, w, c, t * P:(t + 1) * P], xt[:, c, :],
                                  start=(c == 0), stop=(c == KC - 1))
                return last

            def project(dst, w, xt):
                for t in range(TT):
                    for c in range(KC):
                        last = mm(dst[:, t * E:(t + 1) * E], xt[:, c, t * P:(t + 1) * P], w_attn[:, w, c, :],
                                  start=(c == 0), stop=(c == KC - 1))
                return last

            def projections(a, p):
                for s in range(2):
                    b = 2 * p + s
                    B = b + a * BATCH
                    if a == 0:
                        pe.wait_ge(s_ln, ONE + B + 1)
                        pe.wait_ge(s_xT, ONE + B)
                        turn(bank[s], xb[:, s, :, :]).then_inc(s_tx, 1)
                        pe.wait_ge(s_cin[s], 16 * p + 16)
                        pe.wait_ge(s_cT, ONE + B)
                        turn(bank[2 + s], cb[:, s, :, :]).then_inc(s_tc, 1)
                    else:
                        pe.wait_ge(s_src, b + 1)
                        pe.wait_ge(s_xT, ONE + B)
                        turn(bank[s], xb[:, s, :, :]).then_inc(s_tx, 1)
                for s in range(2):
                    B = 2 * p + s + a * BATCH
                    src = xT if a else cT
                    pe.wait_ge(s_xT, ONE + B + 1)
                    pe.wait_ge(s_hi["q"], ONE + B)
                    project_t(bank[4], 4 * a, xT[:, s, :, :]).then_inc(s_proj["q"], 1)
                    if a == 0:
                        pe.wait_ge(s_cT, ONE + B + 1)
                    pe.wait_ge(s_hi["k"], ONE + B)
                    project_t(bank[5], 4 * a + 1, src[:, s, :, :]).then_inc(s_proj["k"], 1)
                    pe.wait_ge(s_v, ONE + B)
                    project(bank[6], 4 * a + 2, src[:, s, :, :]).then_inc(s_proj["v"], 1)

            def max_scores(U, g, i, b, s, r, a):
                h, n = GH * g + i, GH * U + i
                if i == 0 and g % 2 == 0:
                    pe.wait_ge(s_stack[s][g // 2], 16 * STACK_LOADS * (r + a * BATCH // 2 + 1))
                if not isinstance(n, int) or n >= 2:
                    pe.wait_ge(s_max, n - 1)
                for t in range(TT):
                    dst = bank[i % 2][:, t * SEQ:(t + 1) * SEQ]
                    last = mm(dst, stack_q[0:SHIFT_ROW, s, h, t * P:(t + 1) * P], stack_k[0:SHIFT_ROW, s, h, :],
                              start=True, stop=(a == 1))
                    if a == 0:
                        last = mm(dst, ident_bf[:, :], bias_all[:, b * TT + t, :], start=False, stop=True)
                last.then_inc(s_mm, 1)

            def turn_max(U):
                pe.wait_ge(s_max, GH * (U + 1))
                pe.wait_ge(s_ntc, ONE + U)
                nc.tensor.transpose(bank[5][0:GH * TT, 0:P // 2].bitcast(BF16), negmax[:, :], ident_bf[:, :]).then_inc(s_nt, 1)

            def scores(U, g, i, b, s, a):
                h, n = GH * g + i, GH * U + i
                if i == 0:
                    pe.wait_ge(s_row, ONE + 16 * (U + 1))
                pe.wait_ge(s_exp, CREDIT + n - 1)
                for k in range(TT):
                    dst = bank[2 + i % 2][:, k * SEQ:(k + 1) * SEQ]
                    last = mm(dst, stack_k[0:SHIFT_ROW + 1, s, h, k * P:(k + 1) * P], stack_q[0:SHIFT_ROW + 1, s, h, :],
                              start=True, stop=(a == 1))
                    if a == 0:
                        for t in range(TT):
                            last = mm(dst[:, t * P:(t + 1) * P], bias_all[:, b * TT + t, k * P:(k + 1) * P], ident_bf[:, :],
                                      start=False, stop=(t == TT - 1))
                last.then_inc(s_sc, 1)

            def values(U, g):
                pe.wait_ge(s_exp, CREDIT + GH * (U + 1))
                pe.wait_ge(s_vones, U + 1)
                pe.wait_ge(s_oraw, ONE + U)
                for k in range(TT):
                    for i in range(GH):
                        last = mm(bank[4][32 * i:32 * i + 32, 0:SEQ], v_ones[:, k, GH * g + i, :],
                                  probs[:, g % 2, i, k * SEQ:(k + 1) * SEQ], start=(k == 0), stop=(k == TT - 1))
                last.then_inc(s_pv, 1)

            def turn_out(U):
                pe.wait_ge(s_oraw, ONE + U + 1)
                pe.wait_ge(s_on, ONE + U)
                for t in range(TT):
                    last = nc.tensor.transpose(bank[6][:, t * P:(t + 1) * P], o_raw[:, t * P:(t + 1) * P], ident[:, :])
                last.then_inc(s_ot, 1)

            def turn_normalised(B):
                pe.wait_ge(s_on, ONE + 4 * (B + 1))
                pe.wait_ge(s_x1, B)
                turn(bank[7], o_norm).then_inc(s_t2, 1)

            def project_out(B, a):
                pe.wait_ge(s_oT, B + 1)
                project(bank[7], 4 * a + 3, o_t).then_inc(s_wo, 1)

            def attention(a):
                def unit(b, g, s, r, first, ahead):
                    B = b + a * BATCH
                    U = 4 * B + g
                    b2, g2, s2, r2 = two_ahead(b, g, s, r)
                    for i in range(GH):
                        scores(U, g, i, b, s, a)
                        if ahead:
                            max_scores(U + 2, g2, i, b2, s2, r2, a)
                        if i == 1:
                            if g == 1 and not first:
                                turn_normalised(B - 1)
                            if not (first and g == 0):
                                values(U - 1, (g - 1) % GROUPS)
                    if g == 1 and not first:
                        project_out(B - 1, a)
                    if ahead:
                        turn_max(U + 2)
                    if not (first and g == 0):
                        turn_out(U - 1)

                for g in range(2):
                    for i in range(GH):
                        max_scores(4 * a * BATCH + g, g, i, 0, 0, 0, a)
                    turn_max(4 * a * BATCH + g)
                each_unit(pe, unit)
                B = (a + 1) * BATCH - 1
                values(4 * B + 3, 3)
                turn_out(4 * B + 3)
                turn_normalised(B)
                project_out(B, a)

            for a in range(2):
                if a == 1:
                    pe.wait_ge(s_end, ONE + BATCH)
                with pe.Fori(0, BATCH // 2) as p:
                    projections(a, p)
                pe.wait_ge(s_v, ONE + BATCH * (a + 1))
                pe.wait_ge(s_hi["q"], ONE + BATCH * (a + 1))
                pe.wait_ge(s_hi["k"], ONE + BATCH * (a + 1))
                if a == 0:
                    pe.wait_ge(s_bias, BATCH)
                attention(a)

            pe.wait_ge(s_end, ONE + 2 * BATCH)
            flat_oh = onehot[:, :, :].rearrange("p e t -> p (e t)")
            pe.wait_ge(s_oh, 1)
            mm(bank[0][:, 0:EXPERTS * TILES], tri_ones[:, 0, :], flat_oh, start=True, stop=True)
            mm(bank[0][:, EXPERTS * TILES:2 * EXPERTS * TILES], tri_ones[:, 1, :], flat_oh, start=True, stop=True).then_inc(s_rank, 1)
            pe.wait_ge(s_eof, 1)
            pe.wait_ge(s_wts, 32)

            def expert(j):
                return pe.value_load(expert_of[0:1, bass.ds(j, 1)], min_val=0, max_val=EXPERTS - 1)

            def turn_x(j):
                pe.wait_ge(s_xg, 16 * (j + 1))
                for c in range(KC):
                    last = nc.tensor.transpose(bank[7][:, c * P:(c + 1) * P], xg[:, c * P:(c + 1) * P], ident[:, :])
                last.then_inc(s_gx, 1)

            def first_layer(j):
                e = expert(j)
                pe.wait_ge(s_gxT, j + 1)
                for n in range(2):
                    for c in range(KC):
                        last = mm(bank[1 + n][:, :], xg_t[:, c, :], w1[:, e, c, n * 512:(n + 1) * 512],
                                  start=(c == 0), stop=(c == KC - 1))
                    last.then_inc(s_h, 1)

            def turn_hidden(j):
                for n in range(2):
                    pe.wait_ge(s_hb, 2 * j + n + 1)
                    for m in range(4):
                        k = 4 * n + m
                        last = nc.tensor.transpose(bank[3 + n][:, m * P:(m + 1) * P], hid[:, k * P:(k + 1) * P], ident[:, :])
                    last.then_inc(s_ht, 1)

            def second_layer(j):
                e = expert(j)
                pe.wait_ge(s_yb, ONE + j)
                for m in range(MC):
                    if m % 4 == 0:
                        pe.wait_ge(s_hT, 2 * j + m // 4 + 1)
                    last = mm(bank[5][:, 0:E], hid_t[:, m, :], w2[:, e, m, :], start=(m == 0), stop=(m == MC - 1))
                last.then_inc(s_y, 1)

            turn_x(0)
            first_layer(0)
            with pe.Fori(0, SORTED - 1) as j:
                turn_hidden(j)
                turn_x(j + 1)
                first_layer(j + 1)
                second_layer(j)
            turn_hidden(SORTED - 1)
            second_layer(SORTED - 1)

        @block.scalar
        def _(act):
            act.sem_inc(s_xT, ONE)
            act.sem_inc(s_cT, ONE)
            act.sem_inc(s_hi["q"], ONE)
            act.sem_inc(s_hi["k"], ONE)
            act.sem_inc(s_oraw, ONE)
            act.sem_inc(s_mid["q"], ONE)
            act.sem_inc(s_mid["k"], ONE)
            act.wait_ge(s_const, 16 * N_CONST)
            act.wait_ge(s_ident, 1)
            act.sem_inc(s_exp, CREDIT)
            act.sem_inc(s_pv, CREDIT)
            act.sem_inc(s_proj["v"], CREDIT)

            def projections(a, p):
                for s in range(2):
                    B = 2 * p + s + a * BATCH
                    act.wait_ge(s_tx, B + 1)
                    act.wait_ge(s_proj["v"], CREDIT + B - 1)
                    nc.scalar.activation(xT[:, s, :, :].rearrange("p t e -> p (t e)"), bank[s][:, :], ACT.Copy).then_inc(s_xT, 1)
                    if a == 0:
                        act.wait_ge(s_tc, B + 1)
                        nc.scalar.activation(cT[:, s, :, :].rearrange("p t e -> p (t e)"), bank[2 + s][:, :], ACT.Copy).then_inc(s_cT, 1)
                for s in range(2):
                    B = 2 * p + s + a * BATCH
                    for o in "qk":
                        act.wait_ge(s_proj[o], B + 1)
                        act.wait_ge(s_rest[o], ONE + B)
                        act.wait_ge(s_stored[o], ONE + 16 * B)
                        for t in range(KC):
                            bias = bias_qk[:, OPS[o], t:t + 1] if a else 0.0
                            if a and o == "q":
                                bias = bias_q_scaled[:, t:t + 1]
                            ps = bank[4 + OPS[o]][:, t * SEQ:(t + 1) * SEQ]
                            f = nc.scalar.activation(full[:, OPS[o], t, :], ps, ACT.Identity, bias=bias, scale=SCALE if o == "q" else 1.0)
                            hi = nc.scalar.activation(parts[:, OPS[o], 0, t, :], ps, ACT.Identity, bias=bias, scale=SCALE if o == "q" else 1.0)
                        f.then_inc(s_full[o], 1)
                        hi.then_inc(s_hi[o], 1)
                    for o in "qk":
                        act.wait_ge(s_rest[o], ONE + B + 1)
                        nc.scalar.activation(parts[:, OPS[o], 1, :, :], rest[:, OPS[o], :, :], ACT.Copy).then_inc(s_mid[o], 1)

            def read_out(U):
                act.wait_ge(s_pv, CREDIT + U + 1)
                act.wait_ge(s_ot, ONE + U)
                nc.scalar.activation(o_raw[:, :], bank[4][:, 0:SEQ], ACT.Copy).then_inc(s_oraw, 1)

            def copy_normalised(B):
                act.wait_ge(s_t2, ONE + B + 1)
                nc.scalar.activation(o_t[:, :, :].rearrange("p t e -> p (t e)"), bank[7][:, :], ACT.Copy).then_inc(s_oT, 1)

            def attention(a):
                def unit(b, g, s, r, first, ahead):
                    B = b + a * BATCH
                    U = 4 * B + g
                    act.wait_ge(s_pv, CREDIT + U - 1)
                    for i in range(GH):
                        act.wait_ge(s_sc, GH * U + i + 1)
                        nc.scalar.activation(probs[:, g % 2, i, :], bank[2 + i % 2][:, :], ACT.Exp).then_inc(s_exp, 1)
                        if i == 1 and g == 1 and not first:
                            copy_normalised(B - 1)
                        if i == 2 and not (first and g == 0):
                            read_out(U - 1)

                each_unit(act, unit)
                B = (a + 1) * BATCH - 1
                read_out(4 * B + 3)
                copy_normalised(B)

            for a in range(2):
                with act.Fori(0, BATCH // 2) as p:
                    projections(a, p)
                attention(a)

            def copy_x(j):
                act.wait_ge(s_gx, j + 1)
                nc.scalar.activation(xg_t, bank[7][:, 0:KC * P].rearrange("p (c t) -> p c t", c=KC), ACT.Copy).then_inc(s_gxT, 1)

            def relu(j):
                for n in range(2):
                    act.wait_ge(s_ht, 2 * j + n + 1)
                    nc.scalar.activation(hid_t[:, 4 * n:4 * n + 4, :], bank[3 + n][:, :].rearrange("p (m t) -> p m t", m=4), ACT.Relu).then_inc(s_hT, 1)

            copy_x(0)
            with act.Fori(0, SORTED - 1) as j:
                relu(j)
                copy_x(j + 1)
            relu(SORTED - 1)

        @block.gpsimd
        def _(pool):
            pool.sem_inc(s_rest["q"], ONE)
            pool.sem_inc(s_rest["k"], ONE)
            pool.sem_inc(s_lo["q"], ONE)
            pool.sem_inc(s_lo["k"], ONE)
            pool.memset(stack_k[SHIFT_ROW:SHIFT_ROW + 1, :, :, :], 1.0).then_inc(s_ones, 1)
            pool.wait_ge(s_ones, 1)
            pool.memset(v_ones[:, :, :, :], 1.0).then_inc(s_ones, 1)

            pool.memset(neg_half[:, :], -0.5).then_inc(s_ones, 1)

            def inverse_root(n):
                pool.wait_ge(s_vareps, n + 1)
                pool.wait_ge(s_ln, ONE + n)
                pool.tensor_tensor(rstd[:, :], var_eps[:, :], neg_half[:, :], ALU.pow).then_inc(s_rstd, 1)

            def split(B):
                for o in "qk":
                    n = OPS[o]
                    pool.wait_ge(s_full[o], B + 1)
                    pool.wait_ge(s_hi[o], ONE + B + 1)
                    pool.wait_ge(s_lo[o], ONE + B)
                    pool.tensor_tensor(rest[:, n, :, :], full[:, n, :, :], parts[:, n, 0, :, :], ALU.subtract).then_inc(s_rest[o], 1)
                for o in "qk":
                    n = OPS[o]
                    pool.wait_ge(s_mid[o], ONE + B + 1)
                    pool.tensor_tensor(parts[:, n, 2, :, :], rest[:, n, :, :], parts[:, n, 1, :, :], ALU.subtract).then_inc(s_lo[o], 1)

            def spread_v(b, g):
                hs = slice(GH * HD * g, GH * HD * (g + 1))
                pool.tensor_copy(v_ones[:, :, GH * g:GH * g + GH, 0:HD],
                                 v_all[:, tiles(b), hs].rearrange("p t (h d) -> p t h d", h=GH)).then_inc(s_vones, 1)

            pool.wait_ge(s_const, 16 * N_CONST)
            pool.wait_ge(s_ones, 3)
            for a in range(2):
                with pool.Fori(0, BATCH // 2) as p:
                    if a == 0:
                        for s in range(2):
                            inverse_root(2 * p + s)
                    for s in range(2):
                        split(2 * p + s + a * BATCH)
                pool.wait_ge(s_v, ONE + BATCH * (a + 1))
                for g in range(GROUPS):
                    if a == 1:
                        pool.wait_ge(s_pv, CREDIT + 4 * BATCH)
                    spread_v(0, g)

                def residual(b):
                    pool.wait_ge(s_end, ONE + b + a * BATCH)
                    if a == 0:
                        pool.wait_ge(s_xres, 16 * (b + 1))
                        pool.wait_ge(s_x1st, ONE + 16 * b)
                        for t in range(TT):
                            i = pool.tensor_tensor(resid[:, t, :], xres[:, t, :], V["bo0"], ALU.add)
                    else:
                        for t in range(TT):
                            i = pool.tensor_tensor(resid[:, t, :], src_all[:, b * TT + t, :], V["bo1"], ALU.add)
                    i.then_inc(s_res, 1)

                def batch(b, first, last):
                    B = b + a * BATCH
                    for g in range(GROUPS):
                        if g == 1 and not first:
                            inverse_root(BATCH + B - 1)
                        if g == 2:
                            residual(b)
                        if not last:
                            pool.wait_ge(s_pv, CREDIT + 4 * B + g + 1)
                            spread_v(b + 1, g)

                if a == 1:
                    pool.wait_ge(s_x1st, ONE + 16 * BATCH)
                batch(0, True, False)
                with pool.Fori(1, BATCH - 1) as b:
                    batch(b, False, False)
                batch(BATCH - 1, False, True)
                inverse_root(BATCH + (a + 1) * BATCH - 1)

            pool.wait_ge(s_filled, ONE + 16 * SORTED)
            pool.wait_ge(s_place, 1)
            for t in range(TILES):
                pool.indirect_dma_start(sorted_x, bass.IndirectOffsetOnAxis(place[:, t:t + 1], 0), src_all[:, t, :], None,
                                        bounds_check=SORTED * P - 1, oob_is_err=False).then_inc(s_scat, 16)
            with pool.Fori(0, SORTED) as j:
                inverse_root(3 * BATCH + j)
            pool.wait_ge(s_scat, 16 * TILES)
            pool.wait_ge(s_zst, ONE + 16 * SORTED)
            for t in range(TILES):
                pool.indirect_dma_start(src_all[:, t, :], None, sorted_z, bass.IndirectOffsetOnAxis(place[:, t:t + 1], 0),
                                        bounds_check=SORTED * P - 1, oob_is_err=False).then_inc(s_gath[t], 16)

        @block.vector
        def _(dve):
            dve.sem_inc(s_v, ONE)
            dve.sem_inc(s_ntc, ONE)
            dve.sem_inc(s_on, ONE)
            dve.sem_inc(s_end, ONE)
            dve.sem_inc(s_ln, ONE)
            dve.sem_inc(s_yb, ONE)
            step = [0]

            def link(ins):
                step[0] += 1
                ins.then_inc(s_step, 1)
                dve.wait_ge(s_step, step[0])

            nc.vector.memset(x2s[:, :, :], 0.0).then_inc(s_zero, 1)
            dve.wait_ge(s_const, 16 * N_CONST)
            link(nc.vector.tensor_copy(ident_bf[:, :], ident[:, :]))
            nc.vector.tensor_scalar(bias_q_scaled[:, :], bias_qk[:, 0, :], SCALE, None, ALU.mult).then_inc(s_ident, 1)

            def norm_stats(n, src, tiles):
                for t in range(tiles):
                    i = nc.vector.bn_stats(stats[:, t, :], src(t))
                i.then_inc(s_stats, 1)

            def norm_aggregate(n, tiles):
                dve.wait_ge(s_stats, n + 1)
                dve.sem_inc(s_gate, 1)
                for t in range(tiles):
                    i = nc.vector.bn_aggr(mv[:, t, :], stats[:, t, :])
                i.then_inc(s_aggr, 1)
                dve.wait_ge(s_aggr, n + 1)
                nc.vector.tensor_scalar(var_eps[:, :], mv[:, :, 1], EPS, None, ALU.add).then_inc(s_vareps, 1)

            def norm_apply(n, src, dst, tiles):
                dve.wait_ge(s_rstd, n + 1)
                for t in range(tiles):
                    i = nc.vector.tensor_scalar(dst(t), src(t), mv[:, t, 0:1], rstd[:, t:t + 1], ALU.subtract, ALU.mult)
                i.then_inc(s_ln, 1)

            def layer_norm(n, src, dst, tiles=TT):
                norm_stats(n, src, tiles)
                norm_aggregate(n, tiles)
                norm_apply(n, src, dst, tiles)

            def take_v(a, b):
                B = b + a * BATCH
                dve.wait_ge(s_proj["v"], CREDIT + B + 1)
                for t in range(TT):
                    ps = bank[6][:, t * E:(t + 1) * E]
                    if a:
                        i = nc.vector.tensor_tensor(v_all[:, b * TT + t, :], ps, V["bv1"], ALU.add)
                    else:
                        i = nc.vector.tensor_copy(v_all[:, b * TT + t, :], ps)
                i.then_inc(s_v, 1)

            def projections0(p):
                for s in range(2):
                    b = 2 * p + s
                    dve.wait_ge(s_xin[s], 16 * p + 16)
                    layer_norm(b, lambda t: xb[:, s, t, :], lambda t: xb[:, s, t, :])
                for s in range(2):
                    b = 2 * p + s
                    dve.wait_ge(s_min[s], 16 * p + 16)
                    nc.vector.tensor_reduce(seen[:, tiles(b)], mask_u8[:, s, :, :], AX.X, ALU.max)
                    nc.vector.tensor_scalar(bias_all[:, tiles(b), :], mask_u8[:, s, :, :], MASKED, -MASKED, ALU.mult, ALU.add).then_inc(s_bias, 1)
                    take_v(0, b)

            with dve.Fori(0, BATCH // 2) as p:
                projections0(p)
            dve.wait_ge(s_bias, BATCH)
            link(nc.vector.tensor_tensor(seen[:, :], seen[:, :], pad_sb[:, :], ALU.mult))
            link(nc.vector.reciprocal(nan_all[:, :], seen[:, :]))
            link(nc.vector.tensor_scalar(nan_all[:, :], nan_all[:, :], 0.0, None, ALU.mult))

            def max_head(U, i):
                n = GH * U + i
                dve.wait_ge(s_mm, n + 1)
                if i == 0:
                    dve.wait_ge(s_nt, ONE + U)
                nc.vector.tensor_reduce(negmax[:, TT * i:TT * i + TT], bank[i % 2][:, :].rearrange("p (t k) -> p t k", t=TT),
                                        AX.X, ALU.max, negate=True).then_inc(s_max, 1)

            def copy_max(U):
                dve.wait_ge(s_nt, ONE + U + 1)
                dve.wait_ge(s_row, ONE + 16 * U)
                nc.vector.tensor_copy(negmax_t[:, :], bank[5][0:GH * TT, 0:P // 2].bitcast(BF16)).then_inc(s_ntc, 1)

            def normalise(U, g, B):
                dve.wait_ge(s_ot, ONE + U + 1)
                o4 = bank[6][:, 0:TT * P].rearrange("p (t h d) -> p t h d", t=TT, h=GH)
                nc.vector.reciprocal(rden[:, :, :], o4[:, :, :, HD]).then_inc(s_rden, 1)
                dve.wait_ge(s_rden, U + 1)
                if g == 0:
                    dve.wait_ge(s_t2, ONE + B)
                for t in range(TT):
                    i = nc.vector.tensor_tensor(o_norm[:, t, GH * HD * g:GH * HD * (g + 1)].rearrange("p (h d) -> p h d", h=GH),
                                                o4[:, t, :, 0:HD], rden[:, t, :].unsqueeze(2).broadcast_to([P, GH, HD]), ALU.mult)
                i.then_inc(s_on, 1)

            def add_residual(B, b, a):
                dve.wait_ge(s_wo, B + 1)
                dve.wait_ge(s_res, B + 1)
                for t in range(TT):
                    ps = bank[7][:, t * E:(t + 1) * E]
                    if a == 0:
                        k = b * TT + t
                        k = slice(k, k + 1) if isinstance(b, int) else bass.ds(k, 1)
                        i = nc.vector.scalar_tensor_tensor(resid[:, t, :], ps, nan_all[:, k], resid[:, t, :], ALU.add, ALU.add)
                    else:
                        i = nc.vector.tensor_tensor(resid[:, t, :], ps, resid[:, t, :], ALU.add)
                i.then_inc(s_x1, 1)

            def end_batch(B, b, a):
                dve.wait_ge(s_ln, ONE + BATCH + B + 1)
                if a == 0:
                    nc.vector.tensor_copy(src_all[:, tiles(b), :], x2s[:, :, :]).then_inc(s_end, 1)
                    return
                for t in range(TT):
                    i = nc.vector.tensor_tensor(x2s[:, t, :], x2s[:, t, :], V["ln1g"], ALU.mult)
                i.then_inc(s_y1, 1)
                dve.wait_ge(s_y1, b + 1)
                for t in range(TT):
                    i = nc.vector.tensor_tensor(x2s[:, t, :], x2s[:, t, :], V["ln1b"], ALU.add)
                i.then_inc(s_y2, 1)
                dve.wait_ge(s_y2, b + 1)
                nc.vector.tensor_copy(src_all[:, tiles(b), :], x2s[:, :, :])
                for t in range(TT):
                    i = nc.vector.tensor_tensor_reduce(resid[:, t, :], x2s[:, t, :], V["rw"], 1.0, 0.0,
                                                       ALU.mult, ALU.add, keys_b[:, t:t + 1])
                i.then_inc(s_keys, 1)
                dve.wait_ge(s_keys, b + 1)
                nc.vector.tensor_copy(keys[:, tiles(b)], keys_b[:, :]).then_inc(s_end, 1)

            def attention(a):
                def end_step(i, B, b):
                    n = BATCH + B
                    if i == 0:
                        add_residual(B, b, a)
                    if i == 1:
                        dve.wait_ge(s_x1, B + 1)
                        norm_stats(n, lambda t: resid[:, t, :], TT)
                    if i == 2:
                        norm_aggregate(n, TT)
                    if i == 3:
                        norm_apply(n, lambda t: resid[:, t, :], lambda t: x2s[:, t, :], TT)
                        end_batch(B, b, a)

                def unit(b, g, s, r, first, ahead):
                    B = b + a * BATCH
                    U = 4 * B + g
                    for i in range(GH):
                        if ahead:
                            max_head(U + 2, i)
                        if g == 2 and not first:
                            end_step(i, B - 1, b - 1)
                    if ahead:
                        copy_max(U + 2)
                    if not (first and g == 0):
                        normalise(U - 1, (g - 1) % GROUPS, B - 1 if g == 0 else B)

                for g in range(2):
                    for i in range(GH):
                        max_head(4 * a * BATCH + g, i)
                    copy_max(4 * a * BATCH + g)
                each_unit(dve, unit)
                B = (a + 1) * BATCH - 1
                normalise(4 * B + 3, 3, B)
                for i in range(4):
                    end_step(i, B, BATCH - 1)

            for a in range(2):
                if a == 1:
                    with dve.Fori(0, BATCH // 2) as p:
                        for s in range(2):
                            b = 2 * p + s
                            dve.wait_ge(s_tx, BATCH + b - 1)
                            nc.vector.tensor_copy(xb[:, s, :, :], src_all[:, tiles(b), :]).then_inc(s_src, 1)
                        for s in range(2):
                            take_v(1, 2 * p + s)
                if a == 0:
                    dve.wait_ge(s_filled, ONE + 16 * SORTED)
                attention(a)

            def floor(dst, src, tmp, whole):
                link(nc.vector.tensor_copy(whole, src))
                link(nc.vector.tensor_copy(dst, whole))
                link(nc.vector.tensor_tensor(tmp, dst, src, ALU.is_gt))
                link(nc.vector.tensor_tensor(dst, dst, tmp, ALU.subtract))

            R = [route[:, i, :] for i in range(6)]
            dve.wait_ge(s_end, ONE + 2 * BATCH)
            link(nc.vector.tensor_scalar(R[0], keys[:, :], rb_sb[:, 0:1], None, ALU.add))
            floor(R[1], R[0], R[2], route_i[:, :])
            link(nc.vector.tensor_scalar(R[3], R[1], 1.0 / EXPERTS, None, ALU.mult))
            floor(R[4], R[3], R[2], route_i[:, :])
            link(nc.vector.tensor_scalar(R[4], R[4], -float(EXPERTS), None, ALU.mult))
            link(nc.vector.tensor_tensor(R[5], R[1], R[4], ALU.add))
            for e in range(EXPERTS - 1):
                link(nc.vector.tensor_scalar(onehot[:, e, :], R[5], float(e), None, ALU.is_equal))
            link(nc.vector.tensor_tensor(R[0], onehot[:, 0, :], onehot[:, 1, :], ALU.add))
            link(nc.vector.tensor_tensor(R[0], R[0], onehot[:, 2, :], ALU.add))
            nc.vector.tensor_scalar(onehot[:, EXPERTS - 1, :], R[0], -1.0, 1.0, ALU.mult, ALU.add).then_inc(s_oh, 1)

            dve.wait_ge(s_rank, 1)
            per_tile = bank[0][:, EXPERTS * TILES:2 * EXPERTS * TILES].rearrange("p (e t) -> p e t", e=EXPERTS)
            in_tile = bank[0][:, 0:EXPERTS * TILES].rearrange("p (e t) -> p e t", e=EXPERTS)
            link(nc.vector.tensor_copy(count_a[:, :, :], per_tile))
            src, dst, k = count_a, count_b, 1
            while k < TILES:
                nc.vector.tensor_copy(dst[:, :, 0:k], src[:, :, 0:k])
                link(nc.vector.tensor_tensor(dst[:, :, k:TILES], src[:, :, k:TILES], src[:, :, 0:TILES - k], ALU.add))
                src, dst, k = dst, src, 2 * k
            total = src[:, :, TILES - 1]
            S = [small[:, i, :] for i in range(6)]
            link(nc.vector.tensor_scalar(S[0], total, float(P - 1), 1.0 / P, ALU.add, ALU.mult))
            floor(S[1], S[0], S[2], small_i[:, :])
            link(nc.vector.memset(S[3], 0.0))
            for e in range(1, EXPERTS):
                link(nc.vector.tensor_tensor(S[3][:, e:e + 1], S[3][:, e - 1:e], S[1][:, e - 1:e], ALU.add))
            T0, T1 = tile_e[:, 0, :], tile_e[:, 1, :]
            link(nc.vector.tensor_scalar(T0, tile_no[:, :], S[3][:, 1:2], None, ALU.is_ge))
            for e in range(2, EXPERTS):
                link(nc.vector.tensor_scalar(T1, tile_no[:, :], S[3][:, e:e + 1], None, ALU.is_ge))
                link(nc.vector.tensor_tensor(T0, T0, T1, ALU.add))
            nc.vector.tensor_copy(expert_of[:, :], T0).then_inc(s_eof, 1)
            link(nc.vector.tensor_scalar(S[4], S[3], float(P), None, ALU.mult))
            link(nc.vector.tensor_tensor(dst[:, :, :], src[:, :, :], per_tile, ALU.subtract))
            link(nc.vector.tensor_tensor(dst[:, :, :], dst[:, :, :], in_tile, ALU.add))
            link(nc.vector.tensor_tensor(dst[:, :, :], dst[:, :, :], S[4].unsqueeze(2).broadcast_to([P, EXPERTS, TILES]), ALU.add))
            link(nc.vector.tensor_tensor(dst[:, :, :], dst[:, :, :], onehot[:, :, :], ALU.mult))
            link(nc.vector.tensor_tensor(R[0], dst[:, 0, :], dst[:, 1, :], ALU.add))
            link(nc.vector.tensor_tensor(R[1], dst[:, 2, :], dst[:, 3, :], ALU.add))
            link(nc.vector.tensor_tensor(R[2], R[0], R[1], ALU.add))
            nc.vector.tensor_copy(place[:, :], R[2]).then_inc(s_place, 1)

            dve.wait_ge(s_eof, 1)
            dve.wait_ge(s_b1in, 16)

            def expert(j):
                return dve.value_load(expert_of[0:1, bass.ds(j, 1)], min_val=0, max_val=EXPERTS - 1)

            def add_b1(j):
                e = expert(j)
                for n in range(2):
                    dve.wait_ge(s_h, 2 * j + n + 1)
                    nc.vector.tensor_tensor(hid[:, n * 512:(n + 1) * 512], bank[1 + n][:, :], b1_sb[:, e, n * 512:(n + 1) * 512], ALU.add).then_inc(s_hb, 1)

            def end_tile(j):
                e = expert(j)
                dve.wait_ge(s_y, j + 1)
                nc.vector.tensor_tensor(z_a, bank[5][:, 0:E], vec[:, e + VECS.index("b2_0"), :], ALU.add).then_inc(s_yb, 1)
                dve.wait_ge(s_yb, ONE + j + 1)
                dve.wait_ge(s_xr, 16 * (j + 1))
                nc.vector.tensor_tensor(z_b, z_a, xr, ALU.add).then_inc(s_yr, 1)
                dve.wait_ge(s_yr, j + 1)
                layer_norm(3 * BATCH + j, lambda t: z_b, lambda t: z_a, 1)
                dve.wait_ge(s_ln, ONE + 3 * BATCH + j + 1)
                nc.vector.tensor_tensor(z_b, z_a, V["ln2g"], ALU.mult).then_inc(s_f1, 1)
                dve.wait_ge(s_f1, j + 1)
                dve.wait_ge(s_zst, ONE + 16 * j)
                nc.vector.tensor_tensor(z_out, z_b, V["ln2b"], ALU.add).then_inc(s_z, 1)

            add_b1(0)
            with dve.Fori(0, SORTED - 1) as j:
                add_b1(j + 1)
                end_tile(j)
            end_tile(SORTED - 1)
            dve.wait_ge(s_x1in, 16)
            for t in range(TILES):
                dve.wait_ge(s_gath[t], 16)
                nc.vector.tensor_tensor(src_all[:, t, :], src_all[:, t, :], x1_all[:, t, :], ALU.add).then_inc(s_outr, 1)


def kernel(**inputs):
    import concourse.bacc as bacc
    from concourse.bass_utils import run_bass_kernel_spmd

    I = {k: np.asarray(v) for k, v in inputs.items()}
    x0, f = "L0_xattn_", "L0_ffn_"

    def by_dim(w):
        return w.reshape(E, HEADS, HD).transpose(0, 2, 1).reshape(E, E)

    w_attn = np.stack([
        by_dim(I[x0 + "Wq"].T), by_dim(I[x0 + "Wk"].T), I[x0 + "Wv"].T, I[x0 + "Wo"].T,
        by_dim(I[f + "Wq"]), by_dim(I[f + "Wk"]), I[f + "Wv"], I[f + "Wo"],
    ])
    vec = np.stack([
        I[x0 + "bo"], I[f + "bv"], I[f + "bo"], I[f + "ln1_g"], I[f + "ln1_b"], I[f + "ln2_g"], I[f + "ln2_b"],
        I[f + "router_w"][:, 0], *I[f + "b2"],
    ])
    bias_qk = np.stack([I[f + n].reshape(HEADS, HD).T.reshape(KC, P) for n in ("bq", "bk")])
    arrays = {
        "x": I["x"].reshape(BATCH * SEQ, E),
        "ctx": I["ctx_1024"].reshape(BATCH * SEQ, E),
        "mask": I["mask_BxSxS2_bf1"].reshape(BATCH * SEQ, SEQ).view(np.uint8),
        "pad": I["mask_BxS2_bf1"].view(np.uint8).reshape(BATCH * TT, P).T,
        "w_attn": w_attn,
        "vec": vec,
        "bias_qk": bias_qk.transpose(2, 0, 1),
        "b1": I[f + "b1"],
        "tri_ones": np.stack([np.triu(np.ones((P, P), np.float32), 1), np.ones((P, P), np.float32)], 1),
        "tile_no": np.arange(SORTED, dtype=np.float32),
        "rb": I[f + "router_b"],
        "w1": I[f + "W1"],
        "w2": I[f + "W2"],
        "ident": np.eye(P, dtype=np.float32),
    }
    nc = bacc.Bacc("TRN2", target_bir_lowering=False, num_devices=1)
    io, given = {}, {}
    for name, a in arrays.items():
        a = np.ascontiguousarray(a)
        given[f"in_{name}"] = a
        io[name] = nc.dram_tensor(f"in_{name}", a.shape, mybir.dt.from_np(a.dtype), kind="ExternalInput").ap()
    io["out"] = nc.dram_tensor("out_x", (BATCH * SEQ, E), F32, kind="ExternalOutput").ap()
    build(nc, io)
    r = run_bass_kernel_spmd(nc, [given], core_ids=[0])
    return r.results[0]["out_x"].reshape(BATCH, SEQ, E)
```

```python
import numpy as np
import concourse.bass as bass
from concourse import mybir
from contextlib import ExitStack

F32 = mybir.dt.float32
BF16 = mybir.dt.bfloat16
U8 = mybir.dt.uint8
I32 = mybir.dt.int32
ALU = mybir.AluOpType
ACT = mybir.ActivationFunctionType
AX = mybir.AxisListType

P = 128
BATCH, SEQ, E = 8, 256, 256
HEADS, HD = 16, 16
DFF, EXPERTS = 1024, 4
TT = SEQ // P
KC = E // P
GROUPS, GH = 4, 4
TERMS = 6
SHIFT_ROW = TERMS * HD
Q_LOADS = ((0, 0, 3), (3, 1, 2), (5, 2, 1))
K_LOADS = ((0, 0, 3), (3, 0, 2), (5, 0, 1))
STACK_LOADS = len(Q_LOADS) + len(K_LOADS)
HALF = HEADS // 2
SCALE = float(HD) ** -0.5
EPS = 1e-5
MASKED = 1e30
CREDIT = 2
ONE = 1
N_CONST = 9
N_LATER = 8
MC = DFF // P
TILES = BATCH * TT
SORTED = (BATCH * SEQ + EXPERTS * (P - 1)) // P
PICKS = 4
NO_TOKEN = 2 * BATCH * SEQ
VECS = ("bo0", "bv1", "bo1", "ln1g", "ln1b", "ln2g", "ln2b", "rw", "b2_0", "b2_1", "b2_2", "b2_3")


def build(nc, io):
    ctx = ExitStack()
    with ctx:
        def sb(name, shape, dt=F32):
            return ctx.enter_context(nc.sbuf_tensor(name, shape, dt))

        def sem(name):
            return ctx.enter_context(nc.semaphore(name))

        def dram(name, shape, dt):
            return nc.dram_tensor(name, shape, dt, kind="Internal").ap()

        w_attn = sb("w_attn", [P, 8, KC, E])
        vec = sb("vec", [P, len(VECS), E])
        ident = sb("ident", [P, P])
        ident_bf = sb("ident_bf", [P, P], BF16)
        bias_qk = sb("bias_qk", [P, 2, KC])
        tri_ones = sb("tri_ones", [P, 2, P])
        rb_sb = sb("rb_sb", [P, 1])
        pad_sb = sb("pad_sb", [P, BATCH * TT], U8)
        w1 = sb("w1", [P, EXPERTS, KC, DFF])
        w2 = sb("w2", [P, EXPERTS, MC, E])
        flat = w1[:, :, :, :].rearrange("p a b c -> p (a b c)")
        SLOT = TT * E

        def view(n, slots):
            return flat[:, n * SLOT:(n + slots) * SLOT]

        xb = view(0, 2).rearrange("p (s t e) -> p s t e", s=2, t=TT)
        cb = view(2, 2).rearrange("p (s t e) -> p s t e", s=2, t=TT)
        xT = view(4, 2).rearrange("p (s t e) -> p s t e", s=2, t=KC)
        cT = view(6, 2).rearrange("p (s t e) -> p s t e", s=2, t=KC)
        full = view(8, 2).rearrange("p (s t e) -> p s t e", s=2, t=KC)
        rest = view(10, 2).rearrange("p (s t e) -> p s t e", s=2, t=KC)
        mask_u8 = sb("mask_u8", [P, 2, TT, SEQ], U8)

        src_all = sb("src_all", [P, BATCH * TT, E])
        v_all = sb("v_all", [P, BATCH * TT, E])
        bias_all = sb("bias_all", [P, BATCH * TT, SEQ], BF16)
        seen = sb("seen", [P, BATCH * TT])
        nan_all = sb("nan_all", [P, BATCH * TT])
        stack_q = sb("stack_q", [P, 2, HEADS, SEQ], BF16)
        stack_k = sb("stack_k", [P, 2, HEADS, SEQ], BF16)
        probs = sb("probs", [P, 2, GH, TT * SEQ])
        parts = probs[:, :, :, :].rearrange("p s h c -> p (s h c)")[:, 0:6 * SLOT].bitcast(BF16).rearrange(
            "p (s o r t e) -> p s o r t e", s=2, o=2, r=3, t=KC)
        v_ones = sb("v_ones", [P, TT, HEADS, 2 * HD])
        negmax = sb("negmax", [P, 2, GH * TT], BF16)
        negmax_t = sb("negmax_t", [GH * TT, P], BF16)
        o_raw = sb("o_raw", [P, SEQ])
        rden = sb("rden", [P, TT, GH])
        o_norm = sb("o_norm", [P, TT, E])
        o_t = sb("o_t", [P, KC, SEQ])
        xres = sb("xres", [P, TT, E])
        resid = sb("resid", [P, TT, E])
        stats = sb("stats", [P, TT, 6])
        mv = sb("mv", [P, TT, 2])
        rstd = sb("rstd", [P, TT])
        var_eps = sb("var_eps", [P, TT])
        neg_half = sb("neg_half", [P, TT])
        keys_b = sb("keys_b", [P, TT])
        keys = sb("keys", [P, BATCH * TT])
        route = sb("route", [P, 6, TILES])
        route_i = sb("route_i", [P, TILES], I32)
        onehot = sb("onehot", [P, EXPERTS, TILES])
        count_a = sb("count_a", [P, EXPERTS, TILES])
        count_b = sb("count_b", [P, EXPERTS, TILES])
        small = sb("small", [P, 6, EXPERTS])
        small_i = sb("small_i", [P, EXPERTS], I32)
        tile_no = sb("tile_no", [P, SORTED])
        tile_e = sb("tile_e", [P, 2, SORTED])
        expert_of = sb("expert_of", [P, SORTED], I32)
        token_of = sb("token_of", [P, SORTED], I32)
        bias_q_scaled = sb("bias_q_scaled", [P, KC])
        x2s = sb("x2s", [P, TT, E])
        iota = sb("iota", [P, P])
        token_no = sb("token_no", [P, 2, TILES])
        near = sb("near", [P, 2, 4], I32)
        in_col = sb("in_col", [P, TILES, SORTED])
        pick = sb("pick", [P, TILES, 2, SORTED], BF16)
        b1_sb = v_all[:, :, :].rearrange("p t e -> p (t e)").rearrange("p (n f) -> p n f", n=EXPERTS)
        sel = probs[:, :, :, :].bitcast(BF16).rearrange("p s h (b e) -> p (s h b) e", e=P)[:, 0:TILES, :]
        hid = stack_q[:, 0, :, :].bitcast(F32).rearrange("p h s -> p (h s)")[:, 0:DFF]
        hid_t = stack_k[:, 0, :, :].bitcast(F32).rearrange("p h s -> p (h s)")[:, 0:DFF].rearrange("p (m t) -> p m t", m=MC)
        xg = xres[:, 0, :]
        xr = xres[:, 1, :]
        xg_t = o_t[:, 0, :].rearrange("p (c t) -> p c t", c=KC)
        z_a, z_b = resid[:, 0, :], resid[:, 1, :]
        z_c = x2s[:, 0, :]
        z_out, x1g = o_norm[:, 0, :], o_norm[:, 1, :]

        bank = [ctx.enter_context(nc.psum_tensor(f"bank{i}", [P, 512], F32)) for i in range(8)]

        q_dram = dram("q_parts", [2 * BATCH, 3, HD, HEADS, SEQ], BF16)
        k_dram = dram("k_parts", [2 * BATCH, 3, HD, HEADS, SEQ], BF16)
        x1_dram = dram("x1_keep", [BATCH * SEQ, E], F32)
        x2_dram = dram("x2_keep", [BATCH * SEQ, E], F32)

        s_const = sem("constants_loaded")
        s_ident_in = sem("ident_loaded")
        s_w0 = [sem(f"first_w_{o}_loaded") for o in "qkv"]
        s_ident = sem("ident_bf_ready")
        s_scaled = sem("bias_q_scaled_ready")
        s_ones = sem("ones_ready")
        s_wts = sem("ffn_weights_loaded")
        s_xin = [sem(f"x_loaded{s}") for s in range(2)]
        s_cin = [sem(f"ctx_loaded{s}") for s in range(2)]
        s_min = [sem(f"mask_loaded{s}") for s in range(2)]
        s_bias = sem("mask_bias_ready")
        s_stats, s_aggr, s_rstd, s_ln = sem("stats_done"), sem("aggr_done"), sem("rstd_done"), sem("ln_done")
        s_tx, s_tc = sem("x_transposed"), sem("ctx_transposed")
        s_xT, s_cT = sem("xT_ready"), sem("cT_ready")
        s_proj = {o: sem(f"{o}_projected") for o in "qkv"}
        s_full = {o: sem(f"{o}_full_ready") for o in "qk"}
        s_hi = {o: sem(f"{o}_hi_ready") for o in "qk"}
        s_rest = {o: sem(f"{o}_rest_ready") for o in "qk"}
        s_mid = {o: sem(f"{o}_mid_ready") for o in "qk"}
        s_lo = {o: sem(f"{o}_lo_ready") for o in "qk"}
        s_stored = [{o: sem(f"{o}_parts_stored{s}") for o in "qk"} for s in range(2)]
        s_v = sem("v_ready")
        s_stack = [[sem(f"stack_loaded{s}{h}") for h in range(2)] for s in range(2)]
        s_row = sem("shift_row_loaded")
        s_vones = sem("v_ones_ready")
        s_mm = sem("max_scores_ready")
        s_max = sem("max_taken")
        s_nt = sem("negmax_transposed")
        s_ntc = sem("negmax_t_ready")
        s_sc = sem("scores_ready")
        s_exp = sem("probs_ready")
        s_pv = sem("pv_done")
        s_oraw = sem("o_raw_ready")
        s_ot = sem("o_raw_transposed")
        s_rden = sem("rden_ready")
        s_on = sem("o_norm_ready")
        s_t2 = sem("o_norm_transposed")
        s_oT = sem("o_t_ready")
        s_wo = sem("out_projected")
        s_xres = sem("xres_loaded")
        s_res = sem("resid_ready")
        s_x1 = sem("x1_ready")
        s_x1st = sem("x1_stored")
        s_end = sem("attention_batch_done")
        s_vareps = sem("var_eps_ready")
        s_gate = sem("stats_gate")
        s_step = sem("vector_step")
        s_keys = sem("router_keys_ready")
        s_x2st = sem("x2_stored")
        s_oh, s_rank = sem("onehot_ready"), sem("ranks_ready")
        s_sel, s_sum = sem("token_picks_ready"), sem("tokens_summed")
        s_ids, s_eof = sem("tokens_of_rows_ready"), sem("tile_experts_ready")
        s_b1in = sem("b1_loaded")
        s_xg, s_xr = sem("sorted_x_loaded"), sem("sorted_residual_loaded")
        s_gx, s_gxT = sem("sorted_x_transposed"), sem("sorted_xT_ready")
        s_h = sem("hidden_psum_ready")
        s_hb = sem("hidden_biased")
        s_ht = sem("hidden_transposed")
        s_hT = sem("hidden_t_ready")
        s_y = sem("expert_out_ready")
        s_yb = sem("expert_out_biased")
        s_yr = sem("ffn_residual_added")
        s_z, s_zst = sem("z_ready"), sem("z_stored")
        s_x1g = sem("x1_gathered")
        s_near = sem("near_rows_copied")
        s_held = sem("transfer_gate")
        s_src = sem("src_staged")
        s_y1, s_y2 = sem("ln1_scaled"), sem("x2_ready")
        s_f1, s_f2 = sem("ln2_scaled"), sem("ln2_shifted")

        x_d, c_d, m_d, out_d = io["x"], io["ctx"], io["mask"], io["out"]
        OPS = {"q": 0, "k": 1}
        V = {n: vec[:, i, :] for i, n in enumerate(VECS)}
        block = ctx.enter_context(nc.Block())

        def tiles(b):
            return slice(b * TT, b * TT + TT) if isinstance(b, int) else bass.ds(b * TT, TT)

        def rows(b):
            return slice(b * SEQ, b * SEQ + SEQ) if isinstance(b, int) else bass.ds(b * SEQ, SEQ)

        def each_unit(eng, unit):
            for g in range(GROUPS):
                unit(0, g, 0, 0, True, True)
            with eng.Fori(0, BATCH // 2 - 1) as p:
                for odd in (1, 0):
                    b, r = 2 * p + 2 - odd, p + 1 - odd
                    for g in range(GROUPS):
                        unit(b, g, odd, r, False, True)
            for g in range(GROUPS):
                unit(BATCH - 1, g, 1, BATCH // 2 - 1, False, g < 2)

        def one_ahead(b, g, s):
            return (b, g + 1, s) if g < 3 else (b + 1, 0, 1 - s)

        def is_last(b, g):
            return isinstance(b, int) and b == BATCH - 1 and g == GROUPS - 1

        def two_ahead(b, g, s, r):
            return (b, g + 2, s, r) if g < 2 else (b + 1, g - 2, 1 - s, r + s)

        @block.sync
        def _(sp):
            sp.sem_inc(s_row, ONE)
            sp.sem_inc(s_x1st, ONE)
            sp.sem_inc(s_x2st, ONE)
            for s in range(2):
                for o in "qk":
                    sp.sem_inc(s_stored[s][o], ONE)
            def load_x_in(b, s):
                sp.dma_start(xb[:, s, :, :], x_d[rows(b), :].rearrange("(t p) e -> p t e", p=P)).then_inc(s_xin[s], 16)

            def load_ctx(b, s):
                sp.dma_start(cb[:, s, :, :], c_d[rows(b), :].rearrange("(t p) e -> p t e", p=P)).then_inc(s_cin[s], 16)

            def load_mask(b, s):
                sp.dma_start(mask_u8[:, s, :, :], m_d[rows(b), :].rearrange("(t p) e -> p t e", p=P)).then_inc(s_min[s], 16)

            def load_w(n):
                sp.dma_start(w_attn[:, n, :, :], io["w_attn"][n].rearrange("(c p) e -> p c e", p=P)).then_inc(s_const, 16)

            def load_vec(n0, n1):
                sp.dma_start(vec[:, n0:n1, :], io["vec"][n0:n1].partition_broadcast(P)).then_inc(s_const, 16)

            def store_parts(B, s):
                for o in "qk":
                    sp.wait_ge(s_mid[o], ONE + B + 1)
                    sp.wait_ge(s_lo[o], ONE + B + 1)
                    dst = (q_dram if o == "q" else k_dram)[B]
                    sp.dma_start(dst.rearrange("r (t d) h k -> (d h) r t k", t=KC), parts[:, s, OPS[o], :, :, :]).then_inc(s_stored[s][o], 16)

            def load_stack(B, s, half):
                hs = slice(HALF * half, HALF * half + HALF)
                for r, part, n in Q_LOADS:
                    sp.dma_start(stack_q[HD * r:HD * (r + n), s, hs, :],
                                 q_dram[B, part:part + 1, :, hs, :].to_broadcast([n, HD, HALF, SEQ])).then_inc(s_stack[s][half], 16)
                for r, p0, n in K_LOADS:
                    sp.dma_start(stack_k[HD * r:HD * (r + n), s, hs, :],
                                 k_dram[B, p0:p0 + n, :, hs, :].rearrange("r d h k -> (r d) h k")).then_inc(s_stack[s][half], 16)

            def load_whole_stack(B, s):
                for r, part, n in Q_LOADS:
                    sp.dma_start(stack_q[HD * r:HD * (r + n), s, :, :],
                                 q_dram[B, part:part + 1, :, :, :].to_broadcast([n, HD, HEADS, SEQ])).then_inc(s_stack[s][0], 16)
                for r, p0, n in K_LOADS:
                    sp.dma_start(stack_k[HD * r:HD * (r + n), s, :, :],
                                 k_dram[B, p0:p0 + n, :, :, :].rearrange("r d h k -> (r d) h k")).then_inc(s_stack[s][0], 16)
                sp.sem_inc(s_stack[s][1], 16 * STACK_LOADS)

            def shift_row(U, g, s):
                sp.wait_ge(s_ntc, ONE + U + 1)
                sp.dma_start(stack_q[SHIFT_ROW:SHIFT_ROW + 1, s, GH * g:GH * g + GH, :].rearrange("o h (t k) -> o (h t) k", t=TT),
                             negmax_t[:, :]).then_inc(s_row, 16)

            def load_xres(b):
                sp.dma_start(xres[:, :, :], x_d[rows(b), :].rearrange("(t p) e -> p t e", p=P)).then_inc(s_xres, 16)

            load_x_in(0, 0)
            sp.dma_start(ident[:, :], io["ident"]).then_inc(s_ident_in, 16)
            load_x_in(1, 1)
            load_ctx(0, 0)
            for n in range(3):
                sp.dma_start(w_attn[:, n, :, :], io["w_attn"][n].rearrange("(c p) e -> p c e", p=P)).then_inc(s_w0[n], 16)
            load_mask(0, 0)
            sp.dma_start(bias_qk[:, :, :], io["bias_qk"]).then_inc(s_const, 16)
            load_ctx(1, 1)
            load_mask(1, 1)
            sp.dma_start(tri_ones[:, :, :], io["tri_ones"]).then_inc(s_const, 16)
            sp.dma_start(iota[:, :], io["iota"].partition_broadcast(P)).then_inc(s_const, 16)
            sp.dma_start(token_no[:, :, :], io["token_no"]).then_inc(s_const, 16)
            sp.dma_start(tile_no[:, :], io["tile_no"].partition_broadcast(P)).then_inc(s_const, 16)
            sp.dma_start(rb_sb[:, :], io["rb"].partition_broadcast(P)).then_inc(s_const, 16)
            sp.dma_start(pad_sb[:, :], io["pad"]).then_inc(s_const, 16)
            load_w(3)
            load_vec(0, 1)
            for a in range(2):
                B0 = a * BATCH
                if a == 0:
                    def step(b, s):
                        sp.wait_ge(s_tx, b + 1)
                        load_x_in(b + 2, s)
                        sp.wait_ge(s_tc, b + 1)
                        load_ctx(b + 2, s)
                        if not (isinstance(b, int) and b == 0):
                            store_parts(b - 1, 1 - s)
                        sp.wait_ge(s_bias, b + 1)
                        load_mask(b + 2, s)

                    for b in range(2):
                        step(b, b)
                    with sp.Fori(1, BATCH // 2 - 1) as p:
                        for s in range(2):
                            step(2 * p + s, s)
                    store_parts(BATCH - 3, 1)
                else:
                    with sp.Fori(0, BATCH // 2 - 1) as p:
                        for s in range(2):
                            store_parts(2 * p + s + BATCH, s)
                for s in range(2):
                    for o in "qk":
                        sp.wait_ge(s_stored[s][o], ONE + 16 * (B0 // 2 + 1))
                    load_whole_stack(B0 + s, s)
                    store_parts(B0 + BATCH - 2 + s, s)
                if a == 0:
                    load_xres(0)
                else:
                    sp.wait_ge(s_proj["v"], CREDIT + 2 * BATCH)
                shift_row(4 * B0, 0, 0)
                for s in range(2):
                    for o in "qk":
                        sp.wait_ge(s_stored[s][o], ONE + 16 * (a + 1) * BATCH // 2)

                def unit(b, g, s, r, first, ahead):
                    B = b + B0
                    U = 4 * B + g
                    if not is_last(b, g):
                        _, g1, s1 = one_ahead(b, g, s)
                        shift_row(U + 1, g1, s1)
                    if g < 2 and not isinstance(b, int):
                        load_stack(B + 1, 1 - s, g)
                    if a == 0 and g == 1 and not first:
                        sp.wait_ge(s_res, B)
                        load_xres(b)
                    if a == 0 and g == 3 and not first:
                        store_x1(b - 1)
                    if a == 1 and g == 3 and not first:
                        store_x2(b - 1)
                    if a == 0 and first:
                        load_w(4 + g)
                        n = len(VECS) // GROUPS
                        load_vec(max(g * n, 1), g * n + n)
                    dst, src = (w2[:, r, 4 * s:4 * s + 4, :], io["w2"][r, 4 * s * P:4 * (s + 1) * P, :].rearrange("(c p) e -> p c e", p=P)) \
                        if a == 0 else (w1[:, r, s, :], io["w1"][r, s * P:(s + 1) * P, :])
                    if g == 2:
                        sp.dma_start(dst, src).then_inc(s_wts, 16)

                def store_x2(b):
                    sp.wait_ge(s_y2, b + 1)
                    sp.dma_start(x2_dram[rows(b), :].rearrange("(t p) e -> p t e", p=P), x2s[:, :, :]).then_inc(s_x2st, 16)

                def store_x1(b):
                    sp.wait_ge(s_x1, b + 1)
                    sp.dma_start(x1_dram[rows(b), :].rearrange("(t p) e -> p t e", p=P), resid[:, :, :]).then_inc(s_x1st, 16)

                each_unit(sp, unit)
                if a == 0:
                    store_x1(BATCH - 1)
                else:
                    store_x2(BATCH - 1)

            sp.wait_ge(s_vones, 4 * 2 * BATCH)
            sp.dma_start(b1_sb, io["b1"].partition_broadcast(P)).then_inc(s_b1in, 16)
            sp.wait_ge(s_x1st, ONE + 16 * BATCH)
            sp.wait_ge(s_x2st, ONE + 16 * BATCH)

        @block.tensor
        def _(pe):
            pe.sem_inc(s_nt, ONE)
            pe.sem_inc(s_ot, ONE)
            pe.sem_inc(s_t2, ONE)
            mm = nc.tensor.matmul
            pe.wait_ge(s_ident_in, 16)

            def turn(dst, src):
                for c in range(KC):
                    for t in range(TT):
                        last = nc.tensor.transpose(dst[:, c * SEQ + t * P:c * SEQ + (t + 1) * P], src[:, t, c * P:(c + 1) * P], ident[:, :])
                return last

            def project_t(dst, w, xt):
                for t in range(KC):
                    for c in range(KC):
                        last = mm(dst[:, t * SEQ:(t + 1) * SEQ], w_attn[:, w, c, t * P:(t + 1) * P], xt[:, c, :],
                                  start=(c == 0), stop=(c == KC - 1))
                return last

            def project(dst, w, xt):
                for t in range(TT):
                    for c in range(KC):
                        last = mm(dst[:, t * E:(t + 1) * E], xt[:, c, t * P:(t + 1) * P], w_attn[:, w, c, :],
                                  start=(c == 0), stop=(c == KC - 1))
                return last

            def turn_inputs(a, b, s, p):
                B = b + a * BATCH
                if a == 0:
                    pe.wait_ge(s_ln, ONE + B + 1)
                else:
                    pe.wait_ge(s_src, b + 1)
                pe.wait_ge(s_xT, ONE + B)
                turn(bank[s], xb[:, s, :, :]).then_inc(s_tx, 1)
                if a == 0:
                    pe.wait_ge(s_cin[s], 16 * p + 16)
                    pe.wait_ge(s_cT, ONE + B)
                    turn(bank[2 + s], cb[:, s, :, :]).then_inc(s_tc, 1)

            def project_batch(a, b, s):
                B = b + a * BATCH
                src = xT if a else cT
                pe.wait_ge(s_xT, ONE + B + 1)
                pe.wait_ge(s_hi["q"], ONE + B)
                project_t(bank[4], 4 * a, xT[:, s, :, :]).then_inc(s_proj["q"], 1)
                if a == 0:
                    pe.wait_ge(s_cT, ONE + B + 1)
                pe.wait_ge(s_hi["k"], ONE + B)
                project_t(bank[5], 4 * a + 1, src[:, s, :, :]).then_inc(s_proj["k"], 1)
                pe.wait_ge(s_v, ONE + B)
                project(bank[6], 4 * a + 2, src[:, s, :, :]).then_inc(s_proj["v"], 1)

            def projections(a):
                turn_inputs(a, 0, 0, 0)
                if a == 0:
                    for n in range(3):
                        pe.wait_ge(s_w0[n], 16)
                with pe.Fori(0, BATCH // 2 - 1) as p:
                    for s in range(2):
                        b = 2 * p + s
                        turn_inputs(a, b + 1, 1 - s, p + s)
                        project_batch(a, b, s)
                turn_inputs(a, BATCH - 1, 1, BATCH // 2 - 1)
                project_batch(a, BATCH - 2, 0)
                project_batch(a, BATCH - 1, 1)

            def max_scores(U, g, i, b, s, r, a):
                h, n = GH * g + i, GH * U + i
                if i == 0 and g % 2 == 0:
                    pe.wait_ge(s_stack[s][g // 2], 16 * STACK_LOADS * (r + a * BATCH // 2 + 1))
                if not isinstance(n, int) or n >= 2:
                    pe.wait_ge(s_max, n - 1)
                for t in range(TT):
                    dst = bank[i % 2][:, t * SEQ:(t + 1) * SEQ]
                    last = mm(dst, stack_q[0:SHIFT_ROW, s, h, t * P:(t + 1) * P], stack_k[0:SHIFT_ROW, s, h, :],
                              start=True, stop=(a == 1))
                    if a == 0:
                        last = mm(dst, ident_bf[:, :], bias_all[:, b * TT + t, :], start=False, stop=True)
                last.then_inc(s_mm, 1)

            def turn_max(U, g):
                pe.wait_ge(s_max, GH * (U + 1))
                pe.wait_ge(s_ntc, ONE + U)
                nc.tensor.transpose(bank[5][0:GH * TT, 0:P // 2].bitcast(BF16), negmax[:, g % 2, :], ident_bf[:, :]).then_inc(s_nt, 1)

            def scores(U, g, i, b, s, a):
                h, n = GH * g + i, GH * U + i
                if i == 0:
                    pe.wait_ge(s_row, ONE + 16 * (U + 1))
                pe.wait_ge(s_exp, CREDIT + n - 1)
                for k in range(TT):
                    dst = bank[2 + i % 2][:, k * SEQ:(k + 1) * SEQ]
                    last = mm(dst, stack_k[0:SHIFT_ROW + 1, s, h, k * P:(k + 1) * P], stack_q[0:SHIFT_ROW + 1, s, h, :],
                              start=True, stop=(a == 1))
                    if a == 0:
                        for t in range(TT):
                            last = mm(dst[:, t * P:(t + 1) * P], bias_all[:, b * TT + t, k * P:(k + 1) * P], ident_bf[:, :],
                                      start=False, stop=(t == TT - 1))
                last.then_inc(s_sc, 1)

            def values(U, g):
                pe.wait_ge(s_exp, CREDIT + GH * (U + 1))
                pe.wait_ge(s_vones, U + 1)
                pe.wait_ge(s_oraw, ONE + U)
                for k in range(TT):
                    for i in range(GH):
                        last = mm(bank[4][32 * i:32 * i + 32, 0:SEQ], v_ones[:, k, GH * g + i, :],
                                  probs[:, g % 2, i, k * SEQ:(k + 1) * SEQ], start=(k == 0), stop=(k == TT - 1))
                last.then_inc(s_pv, 1)

            def turn_out(U):
                pe.wait_ge(s_oraw, ONE + U + 1)
                pe.wait_ge(s_on, ONE + U)
                for t in range(TT):
                    last = nc.tensor.transpose(bank[6][:, t * P:(t + 1) * P], o_raw[:, t * P:(t + 1) * P], ident[:, :])
                last.then_inc(s_ot, 1)

            def turn_normalised(B):
                pe.wait_ge(s_on, ONE + 4 * (B + 1))
                pe.wait_ge(s_x1, B)
                turn(bank[7], o_norm).then_inc(s_t2, 1)

            def project_out(B, a):
                pe.wait_ge(s_oT, B + 1)
                project(bank[7], 4 * a + 3, o_t).then_inc(s_wo, 1)

            def attention(a):
                def unit(b, g, s, r, first, ahead):
                    B = b + a * BATCH
                    U = 4 * B + g
                    b2, g2, s2, r2 = two_ahead(b, g, s, r)
                    for i in range(GH):
                        if i == 3 and not (first and g == 0):
                            turn_out(U - 1)
                        if ahead:
                            max_scores(U + 2, g2, i, b2, s2, r2, a)
                        scores(U, g, i, b, s, a)
                        if i == 0 and not is_last(b, g):
                            turn_max(U + 1, (g + 1) % GROUPS)
                        if i == 0 and g == 1 and not first:
                            turn_normalised(B - 1)
                        if i == 3 and g == 1 and not first:
                            project_out(B - 1, a)
                        if i == 1:
                            if not (first and g == 0):
                                values(U - 1, (g - 1) % GROUPS)

                for g in range(2):
                    for i in range(GH):
                        max_scores(4 * a * BATCH + g, g, i, 0, 0, 0, a)
                turn_max(4 * a * BATCH, 0)
                each_unit(pe, unit)
                B = (a + 1) * BATCH - 1
                values(4 * B + 3, 3)
                turn_out(4 * B + 3)
                turn_normalised(B)
                project_out(B, a)

            for a in range(2):
                if a == 1:
                    pe.wait_ge(s_const, 16 * (N_CONST + N_LATER))
                    pe.wait_ge(s_on, ONE + 4 * BATCH)
                projections(a)
                pe.wait_ge(s_v, ONE + BATCH * (a + 1))
                pe.wait_ge(s_hi["q"], ONE + BATCH * (a + 1))
                pe.wait_ge(s_hi["k"], ONE + BATCH * (a + 1))
                if a == 0:
                    pe.wait_ge(s_bias, BATCH)
                    pe.wait_ge(s_const, 16 * N_CONST)
                    pe.wait_ge(s_ident, 1)
                attention(a)

            pe.wait_ge(s_end, ONE + 2 * BATCH)
            flat_oh = onehot[:, :, :].rearrange("p e t -> p (e t)")
            pe.wait_ge(s_oh, 1)
            mm(bank[0][:, 0:EXPERTS * TILES], tri_ones[:, 0, :], flat_oh, start=True, stop=True)
            mm(bank[0][:, EXPERTS * TILES:2 * EXPERTS * TILES], tri_ones[:, 1, :], flat_oh, start=True, stop=True).then_inc(s_rank, 1)
            for t in range(TILES):
                if t % PICKS == 0:
                    pe.wait_ge(s_sel, t // PICKS + 1)
                last = mm(bank[0][:, 0:2 * SORTED], sel[:, t, :], pick[:, t, :, :].rearrange("p n j -> p (n j)"), start=(t == 0), stop=(t == TILES - 1))
            last.then_inc(s_sum, 1)
            pe.wait_ge(s_eof, 1)
            pe.wait_ge(s_wts, 16 * 2 * BATCH)

            def expert(j):
                return pe.value_load(expert_of[0:1, bass.ds(j, 1)], min_val=0, max_val=EXPERTS - 1)

            def turn_x(j):
                pe.wait_ge(s_xg, 16 * (j + 1))
                for c in range(KC):
                    last = nc.tensor.transpose(bank[7][:, c * P:(c + 1) * P], xg[:, c * P:(c + 1) * P], ident[:, :])
                last.then_inc(s_gx, 1)

            def first_layer(j):
                e = expert(j)
                pe.wait_ge(s_gxT, j + 1)
                for n in range(2):
                    for c in range(KC):
                        last = mm(bank[1 + n][:, :], xg_t[:, c, :], w1[:, e, c, n * 512:(n + 1) * 512],
                                  start=(c == 0), stop=(c == KC - 1))
                    last.then_inc(s_h, 1)

            def turn_hidden(j):
                for n in range(2):
                    pe.wait_ge(s_hb, 2 * j + n + 1)
                    for m in range(4):
                        k = 4 * n + m
                        last = nc.tensor.transpose(bank[3 + n][:, m * P:(m + 1) * P], hid[:, k * P:(k + 1) * P], ident[:, :])
                    last.then_inc(s_ht, 1)

            def second_layer(j):
                e = expert(j)
                pe.wait_ge(s_yb, ONE + j)
                for m in range(MC):
                    if m % 4 == 0:
                        pe.wait_ge(s_hT, 2 * j + m // 4 + 1)
                    last = mm(bank[5][:, 0:E], hid_t[:, m, :], w2[:, e, m, :], start=(m == 0), stop=(m == MC - 1))
                last.then_inc(s_y, 1)

            turn_x(0)
            first_layer(0)
            with pe.Fori(0, SORTED - 1) as j:
                turn_x(j + 1)
                turn_hidden(j)
                first_layer(j + 1)
                second_layer(j)
            turn_hidden(SORTED - 1)
            second_layer(SORTED - 1)

        @block.scalar
        def _(act):
            act.sem_inc(s_xT, ONE)
            act.sem_inc(s_cT, ONE)
            act.sem_inc(s_hi["q"], ONE)
            act.sem_inc(s_hi["k"], ONE)
            act.sem_inc(s_oraw, ONE)
            act.sem_inc(s_mid["q"], ONE)
            act.sem_inc(s_mid["k"], ONE)
            act.sem_inc(s_exp, CREDIT)
            act.sem_inc(s_pv, CREDIT)
            act.sem_inc(s_proj["v"], CREDIT)

            def copy_inputs(a, b, s):
                B = b + a * BATCH
                act.wait_ge(s_tx, B + 1)
                act.wait_ge(s_proj["v"], CREDIT + B - 1)
                nc.scalar.activation(xT[:, s, :, :].rearrange("p t e -> p (t e)"), bank[s][:, :], ACT.Copy).then_inc(s_xT, 1)
                if a == 0:
                    act.wait_ge(s_tc, B + 1)
                    nc.scalar.activation(cT[:, s, :, :].rearrange("p t e -> p (t e)"), bank[2 + s][:, :], ACT.Copy).then_inc(s_cT, 1)

            def first_parts(a, b, s, p):
                B = b + a * BATCH
                for o in "qk":
                    act.wait_ge(s_proj[o], B + 1)
                    act.wait_ge(s_rest[o], ONE + B)
                    act.wait_ge(s_stored[s][o], ONE + 16 * (p + a * BATCH // 2))
                    for t in range(KC):
                        bias = bias_qk[:, OPS[o], t:t + 1] if a else 0.0
                        if a and o == "q":
                            bias = bias_q_scaled[:, t:t + 1]
                        ps = bank[4 + OPS[o]][:, t * SEQ:(t + 1) * SEQ]
                        f = nc.scalar.activation(full[:, OPS[o], t, :], ps, ACT.Identity, bias=bias, scale=SCALE if o == "q" else 1.0)
                        hi = nc.scalar.activation(parts[:, s, OPS[o], 0, t, :], ps, ACT.Identity, bias=bias, scale=SCALE if o == "q" else 1.0)
                    f.then_inc(s_full[o], 1)
                    hi.then_inc(s_hi[o], 1)

            def second_parts(a, b, s):
                B = b + a * BATCH
                for o in "qk":
                    act.wait_ge(s_rest[o], ONE + B + 1)
                    nc.scalar.activation(parts[:, s, OPS[o], 1, :, :], rest[:, OPS[o], :, :], ACT.Copy).then_inc(s_mid[o], 1)

            def projections(a):
                copy_inputs(a, 0, 0)
                with act.Fori(0, BATCH // 2 - 1) as p:
                    for s in range(2):
                        b = 2 * p + s
                        copy_inputs(a, b + 1, 1 - s)
                        first_parts(a, b, s, p)
                        second_parts(a, b, s)
                copy_inputs(a, BATCH - 1, 1)
                for s in range(2):
                    first_parts(a, BATCH - 2 + s, s, BATCH // 2 - 1)
                    second_parts(a, BATCH - 2 + s, s)

            def read_out(U):
                act.wait_ge(s_pv, CREDIT + U + 1)
                act.wait_ge(s_ot, ONE + U)
                nc.scalar.activation(o_raw[:, :], bank[4][:, 0:SEQ], ACT.Copy).then_inc(s_oraw, 1)

            def copy_normalised(B):
                act.wait_ge(s_t2, ONE + B + 1)
                nc.scalar.activation(o_t[:, :, :].rearrange("p t e -> p (t e)"), bank[7][:, :], ACT.Copy).then_inc(s_oT, 1)

            def attention(a):
                def unit(b, g, s, r, first, ahead):
                    B = b + a * BATCH
                    U = 4 * B + g
                    act.wait_ge(s_pv, CREDIT + U - 1)
                    for i in range(GH):
                        act.wait_ge(s_sc, GH * U + i + 1)
                        nc.scalar.activation(probs[:, g % 2, i, :], bank[2 + i % 2][:, :], ACT.Exp).then_inc(s_exp, 1)
                        if i == 0 and g == 1 and not first:
                            copy_normalised(B - 1)
                        if i == 1 and not (first and g == 0):
                            read_out(U - 1)

                each_unit(act, unit)
                B = (a + 1) * BATCH - 1
                read_out(4 * B + 3)
                copy_normalised(B)

            for a in range(2):
                if a == 1:
                    act.wait_ge(s_const, 16 * (N_CONST + N_LATER))
                    act.wait_ge(s_scaled, 1)
                projections(a)
                for s in range(2):
                    for o in "qk":
                        act.wait_ge(s_stored[s][o], ONE + 16 * (a + 1) * BATCH // 2)
                attention(a)

            def copy_x(j):
                act.wait_ge(s_gx, j + 1)
                nc.scalar.activation(xg_t, bank[7][:, 0:KC * P].rearrange("p (c t) -> p c t", c=KC), ACT.Copy).then_inc(s_gxT, 1)

            def relu(j):
                for n in range(2):
                    act.wait_ge(s_ht, 2 * j + n + 1)
                    nc.scalar.activation(hid_t[:, 4 * n:4 * n + 4, :], bank[3 + n][:, :].rearrange("p (m t) -> p m t", m=4), ACT.Relu).then_inc(s_hT, 1)

            copy_x(0)
            with act.Fori(0, SORTED - 1) as j:
                copy_x(j + 1)
                relu(j)
            relu(SORTED - 1)

        @block.gpsimd
        def _(pool):
            pool.sem_inc(s_rest["q"], ONE)
            pool.sem_inc(s_rest["k"], ONE)
            pool.sem_inc(s_lo["q"], ONE)
            pool.sem_inc(s_lo["k"], ONE)
            pool.memset(neg_half[:, :], -0.5).then_inc(s_ones, 1)

            def inverse_root(n):
                pool.wait_ge(s_vareps, n + 1)
                pool.wait_ge(s_ln, ONE + n)
                pool.tensor_tensor(rstd[:, :], var_eps[:, :], neg_half[:, :], ALU.pow).then_inc(s_rstd, 1)

            def split(B, s):
                for o in "qk":
                    n = OPS[o]
                    pool.wait_ge(s_full[o], B + 1)
                    pool.wait_ge(s_hi[o], ONE + B + 1)
                    pool.wait_ge(s_lo[o], ONE + B)
                    pool.tensor_tensor(rest[:, n, :, :], full[:, n, :, :], parts[:, s, n, 0, :, :], ALU.subtract).then_inc(s_rest[o], 1)
                for o in "qk":
                    n = OPS[o]
                    pool.wait_ge(s_mid[o], ONE + B + 1)
                    pool.tensor_tensor(parts[:, s, n, 2, :, :], rest[:, n, :, :], parts[:, s, n, 1, :, :], ALU.subtract).then_inc(s_lo[o], 1)

            def spread_v(b, g):
                hs = slice(GH * HD * g, GH * HD * (g + 1))
                pool.tensor_copy(v_ones[:, :, GH * g:GH * g + GH, 0:HD],
                                 v_all[:, tiles(b), hs].rearrange("p t (h d) -> p t h d", h=GH)).then_inc(s_vones, 1)

            pool.wait_ge(s_ones, 1)
            for a in range(2):
                if a == 0:
                    for b in range(2):
                        inverse_root(b)
                    pool.wait_ge(s_rstd, 2)
                    pool.memset(stack_k[SHIFT_ROW:SHIFT_ROW + 1, :, :, :], 1.0).then_inc(s_ones, 1)
                    pool.wait_ge(s_ones, 2)
                    pool.memset(v_ones[:, :, :, :], 1.0).then_inc(s_ones, 1)
                    pool.wait_ge(s_ones, 3)
                with pool.Fori(0, BATCH // 2 - 1) as p:
                    for s in range(2):
                        b = 2 * p + s
                        if a == 0:
                            inverse_root(b + 2)
                        split(b + a * BATCH, s)
                for s in range(2):
                    split(BATCH - 2 + s + a * BATCH, s)
                pool.wait_ge(s_v, ONE + BATCH * (a + 1))
                pool.wait_ge(s_const, 16 * N_CONST)
                for g in range(GROUPS):
                    if a == 1:
                        pool.wait_ge(s_pv, CREDIT + 4 * BATCH)
                    spread_v(0, g)

                def residual(b):
                    pool.wait_ge(s_end, ONE + b + a * BATCH)
                    if a == 0:
                        pool.wait_ge(s_xres, 16 * (b + 1))
                        pool.wait_ge(s_x1st, ONE + 16 * b)
                        for t in range(TT):
                            i = pool.tensor_tensor(resid[:, t, :], xres[:, t, :], V["bo0"], ALU.add)
                    else:
                        for t in range(TT):
                            i = pool.tensor_tensor(resid[:, t, :], src_all[:, b * TT + t, :], V["bo1"], ALU.add)
                    i.then_inc(s_res, 1)

                def scale_shift(b):
                    pool.wait_ge(s_ln, ONE + 2 * BATCH + b + 1)
                    for t in range(TT):
                        k = pool.tensor_tensor(x2s[:, t, :], x2s[:, t, :], V["ln1g"], ALU.mult)
                    k.then_inc(s_y1, 1)
                    pool.wait_ge(s_y1, b + 1)
                    for t in range(TT):
                        k = pool.tensor_tensor(x2s[:, t, :], x2s[:, t, :], V["ln1b"], ALU.add)
                    k.then_inc(s_y2, 1)

                def batch(b, first, last):
                    B = b + a * BATCH
                    for g in range(GROUPS):
                        if g == 2 and not first:
                            inverse_root(BATCH + B - 1)
                            if a == 1:
                                scale_shift(b - 1)
                        if not last:
                            pool.wait_ge(s_pv, CREDIT + 4 * B + g + 1)
                            spread_v(b + 1, g)
                    residual(b)

                if a == 1:
                    pool.wait_ge(s_const, 16 * (N_CONST + N_LATER))
                    pool.wait_ge(s_x1st, ONE + 16 * BATCH)
                batch(0, True, False)
                with pool.Fori(1, BATCH - 1) as b:
                    batch(b, False, False)
                batch(BATCH - 1, False, True)
                inverse_root(BATCH + (a + 1) * BATCH - 1)

            def gather(dst, src, rows_of):
                return pool.indirect_dma_start(dst, None, src, bass.IndirectOffsetOnAxis(rows_of, 0),
                                               bounds_check=BATCH * SEQ - 1, oob_is_err=False)

            def token(j):
                return token_of[:, j:j + 1]

            def waited(j):
                if not isinstance(j, int):
                    pool.sem_inc(s_held, 1)

            def gather_x(j, rows_of):
                if not (isinstance(j, int) and j == 0):
                    pool.wait_ge(s_gx, j)
                waited(j)
                gather(xg, x2_dram, rows_of).then_inc(s_xg, 16)

            def gather_residuals(j, rows_of):
                if not (isinstance(j, int) and j == 0):
                    pool.wait_ge(s_yr, j)
                waited(j)
                gather(xr, x2_dram, rows_of).then_inc(s_xr, 16)
                if not (isinstance(j, int) and j == 0):
                    pool.wait_ge(s_z, j)
                waited(j)
                gather(x1g, x1_dram, rows_of).then_inc(s_x1g, 16)

            def scatter_out(j, rows_of):
                pool.wait_ge(s_z, j + 1)
                waited(j)
                pool.indirect_dma_start(out_d, bass.IndirectOffsetOnAxis(rows_of, 0), z_out, None,
                                        bounds_check=BATCH * SEQ - 1, oob_is_err=False).then_inc(s_zst, 16)

            def window(j, s):
                pool.tensor_copy(near[:, s, :], token_of[:, bass.ds(j - 1, 4)]).then_inc(s_near, 1)
                pool.wait_ge(s_near, j)

            pool.wait_ge(s_ids, 1)
            pool.wait_ge(s_x1st, ONE + 16 * BATCH)
            pool.wait_ge(s_x2st, ONE + 16 * BATCH)
            gather_x(0, token(0))
            gather_x(1, token(1))
            gather_residuals(0, token(0))
            gather_x(2, token(2))
            with pool.Fori(0, (SORTED - 3) // 2) as p:
                for s in range(2):
                    j = 2 * p + s + 1
                    window(j, s)
                    gather_x(j + 2, near[:, s, 3:4])
                    inverse_root(3 * BATCH + j - 1)
                    gather_residuals(j, near[:, s, 1:2])
                    scatter_out(j - 1, near[:, s, 0:1])
            for j in range(SORTED - 2 - (SORTED - 3) % 2, SORTED):
                if j + 2 < SORTED:
                    gather_x(j + 2, token(j + 2))
                inverse_root(3 * BATCH + j - 1)
                gather_residuals(j, token(j))
                scatter_out(j - 1, token(j - 1))
            inverse_root(3 * BATCH + SORTED - 1)
            scatter_out(SORTED - 1, token(SORTED - 1))
            pool.wait_ge(s_zst, 16 * SORTED)

        @block.vector
        def _(dve):
            dve.sem_inc(s_v, ONE)
            dve.sem_inc(s_ntc, ONE)
            dve.sem_inc(s_on, ONE)
            dve.sem_inc(s_end, ONE)
            dve.sem_inc(s_ln, ONE)
            dve.sem_inc(s_yb, ONE)
            step = [0]

            def link(ins):
                step[0] += 1
                ins.then_inc(s_step, 1)
                dve.wait_ge(s_step, step[0])

            dve.wait_ge(s_ident_in, 16)

            def norm_stats(n, src, tiles):
                for t in range(tiles):
                    i = nc.vector.bn_stats(stats[:, t, :], src(t))
                i.then_inc(s_stats, 1)

            def norm_aggregate(n, tiles):
                dve.wait_ge(s_stats, n + 1)
                dve.sem_inc(s_gate, 1)
                for t in range(tiles):
                    i = nc.vector.bn_aggr(mv[:, t, :], stats[:, t, :])
                i.then_inc(s_aggr, 1)
                dve.wait_ge(s_aggr, n + 1)
                nc.vector.tensor_scalar(var_eps[:, :], mv[:, :, 1], EPS, None, ALU.add).then_inc(s_vareps, 1)

            def norm_apply(n, src, dst, tiles):
                dve.wait_ge(s_rstd, n + 1)
                for t in range(tiles):
                    i = nc.vector.tensor_scalar(dst(t), src(t), mv[:, t, 0:1], rstd[:, t:t + 1], ALU.subtract, ALU.mult)
                i.then_inc(s_ln, 1)

            def layer_norm(n, src, dst, tiles=TT):
                norm_stats(n, src, tiles)
                norm_aggregate(n, tiles)
                norm_apply(n, src, dst, tiles)

            def take_v(a, b):
                B = b + a * BATCH
                dve.wait_ge(s_proj["v"], CREDIT + B + 1)
                for t in range(TT):
                    ps = bank[6][:, t * E:(t + 1) * E]
                    if a:
                        i = nc.vector.tensor_tensor(v_all[:, b * TT + t, :], ps, V["bv1"], ALU.add)
                    else:
                        i = nc.vector.tensor_copy(v_all[:, b * TT + t, :], ps)
                i.then_inc(s_v, 1)

            def norm_input(b, s, p):
                dve.wait_ge(s_xin[s], 16 * p + 16)
                layer_norm(b, lambda t: xb[:, s, t, :], lambda t: xb[:, s, t, :])

            def take_mask(b, s, p):
                dve.wait_ge(s_min[s], 16 * p + 16)
                nc.vector.tensor_reduce(seen[:, tiles(b)], mask_u8[:, s, :, :], AX.X, ALU.max)
                nc.vector.tensor_scalar(bias_all[:, tiles(b), :], mask_u8[:, s, :, :], MASKED, -MASKED, ALU.mult, ALU.add).then_inc(s_bias, 1)

            for b in range(2):
                norm_input(b, b, 0)
            nc.vector.tensor_copy(ident_bf[:, :], ident[:, :]).then_inc(s_ident, 1)
            with dve.Fori(0, BATCH // 2 - 1) as p:
                for s in range(2):
                    b = 2 * p + s
                    norm_input(b + 2, s, p + 1)
                    take_mask(b, s, p)
                    take_v(0, b)
            for s in range(2):
                b = BATCH - 2 + s
                take_mask(b, s, BATCH // 2 - 1)
                take_v(0, b)
            dve.wait_ge(s_const, 16 * N_CONST)
            nc.vector.tensor_scalar(bias_q_scaled[:, :], bias_qk[:, 0, :], SCALE, None, ALU.mult).then_inc(s_scaled, 1)
            dve.wait_ge(s_bias, BATCH)
            link(nc.vector.tensor_tensor(seen[:, :], seen[:, :], pad_sb[:, :], ALU.mult))
            link(nc.vector.reciprocal(nan_all[:, :], seen[:, :]))
            link(nc.vector.tensor_scalar(nan_all[:, :], nan_all[:, :], 0.0, None, ALU.mult))

            def max_head(U, g, i):
                n = GH * U + i
                dve.wait_ge(s_mm, n + 1)
                if i == 0 and not (isinstance(U, int) and U < 2):
                    dve.wait_ge(s_nt, ONE + U - 1)
                nc.vector.tensor_reduce(negmax[:, g % 2, TT * i:TT * i + TT], bank[i % 2][:, :].rearrange("p (t k) -> p t k", t=TT),
                                        AX.X, ALU.max, negate=True).then_inc(s_max, 1)

            def copy_max(U):
                dve.wait_ge(s_nt, ONE + U + 1)
                dve.wait_ge(s_row, ONE + 16 * U)
                nc.vector.tensor_copy(negmax_t[:, :], bank[5][0:GH * TT, 0:P // 2].bitcast(BF16)).then_inc(s_ntc, 1)

            def normalise(U, g, B):
                dve.wait_ge(s_ot, ONE + U + 1)
                o4 = bank[6][:, 0:TT * P].rearrange("p (t h d) -> p t h d", t=TT, h=GH)
                nc.vector.reciprocal(rden[:, :, :], o4[:, :, :, HD]).then_inc(s_rden, 1)
                dve.wait_ge(s_rden, U + 1)
                if g == 0:
                    dve.wait_ge(s_t2, ONE + B)
                for t in range(TT):
                    i = nc.vector.tensor_tensor(o_norm[:, t, GH * HD * g:GH * HD * (g + 1)].rearrange("p (h d) -> p h d", h=GH),
                                                o4[:, t, :, 0:HD], rden[:, t, :].unsqueeze(2).broadcast_to([P, GH, HD]), ALU.mult)
                i.then_inc(s_on, 1)

            def add_residual(B, b, a):
                dve.wait_ge(s_wo, B + 1)
                dve.wait_ge(s_res, B + 1)
                for t in range(TT):
                    ps = bank[7][:, t * E:(t + 1) * E]
                    if a == 0:
                        k = b * TT + t
                        k = slice(k, k + 1) if isinstance(b, int) else bass.ds(k, 1)
                        i = nc.vector.scalar_tensor_tensor(resid[:, t, :], ps, nan_all[:, k], resid[:, t, :], ALU.add, ALU.add)
                    else:
                        i = nc.vector.tensor_tensor(resid[:, t, :], ps, resid[:, t, :], ALU.add)
                i.then_inc(s_x1, 1)

            def router_keys(b):
                dve.wait_ge(s_y2, b + 1)
                for t in range(TT):
                    k = nc.vector.tensor_tensor_reduce(resid[:, t, :], x2s[:, t, :], V["rw"], 1.0, 0.0,
                                                       ALU.mult, ALU.add, keys_b[:, t:t + 1])
                k.then_inc(s_keys, 1)
                dve.wait_ge(s_keys, b + 1)
                nc.vector.tensor_copy(keys[:, tiles(b)], keys_b[:, :]).then_inc(s_end, 1)

            def stage_input(b, s):
                dve.wait_ge(s_tx, BATCH + b - 1)
                nc.vector.tensor_copy(xb[:, s, :, :], src_all[:, tiles(b), :]).then_inc(s_src, 1)

            def attention(a):
                def end_step(i, B, b):
                    n = BATCH + B
                    if i == 0:
                        add_residual(B, b, a)
                    if i == 1:
                        dve.wait_ge(s_x1, B + 1)
                        norm_stats(n, lambda t: resid[:, t, :], TT)
                    if i == 2:
                        norm_aggregate(n, TT)
                    if i == 3 and a == 1:
                        dve.wait_ge(s_x2st, ONE + 16 * b)
                        norm_apply(n, lambda t: resid[:, t, :], lambda t: x2s[:, t, :], TT)
                    if i == 3 and a == 0:
                        norm_apply(n, lambda t: resid[:, t, :], lambda t: x2s[:, t, :], TT)
                        dve.wait_ge(s_ln, ONE + BATCH + B + 1)
                        nc.vector.tensor_copy(src_all[:, tiles(b), :], x2s[:, :, :]).then_inc(s_end, 1)

                def unit(b, g, s, r, first, ahead):
                    B = b + a * BATCH
                    U = 4 * B + g
                    for i in range(GH):
                        if i == 3 and not (first and g == 0):
                            normalise(U - 1, (g - 1) % GROUPS, B - 1 if g == 0 else B)
                        if ahead:
                            max_head(U + 2, g, i)
                        if i == 0 and not is_last(b, g):
                            copy_max(U + 1)
                        if g == 2 and not first:
                            end_step(i, B - 1, b - 1)
                    if a == 1 and g == 3 and not first:
                        router_keys(b - 1)

                for g in range(2):
                    for i in range(GH):
                        max_head(4 * a * BATCH + g, g, i)
                copy_max(4 * a * BATCH)
                each_unit(dve, unit)
                B = (a + 1) * BATCH - 1
                normalise(4 * B + 3, 3, B)
                if a == 0:
                    for b in range(2):
                        stage_input(b, b)
                for i in range(4):
                    end_step(i, B, BATCH - 1)
                if a == 1:
                    dve.wait_ge(s_ln, ONE + BATCH + B + 1)
                    for t in range(TT):
                        k = nc.vector.tensor_tensor(x2s[:, t, :], x2s[:, t, :], V["ln1g"], ALU.mult)
                    k.then_inc(s_y1, 1)
                    dve.wait_ge(s_y1, BATCH)
                    for t in range(TT):
                        k = nc.vector.tensor_tensor(x2s[:, t, :], x2s[:, t, :], V["ln1b"], ALU.add)
                    k.then_inc(s_y2, 1)
                    router_keys(BATCH - 1)

            for a in range(2):
                if a == 1:
                    dve.wait_ge(s_const, 16 * (N_CONST + N_LATER))
                    with dve.Fori(0, BATCH // 2 - 1) as p:
                        for s in range(2):
                            b = 2 * p + s
                            stage_input(b + 2, s)
                            take_v(1, b)
                    for b in (BATCH - 2, BATCH - 1):
                        take_v(1, b)
                attention(a)

            def floor(dst, src, tmp, whole):
                link(nc.vector.tensor_copy(whole, src))
                link(nc.vector.tensor_copy(dst, whole))
                link(nc.vector.tensor_tensor(tmp, dst, src, ALU.is_gt))
                link(nc.vector.tensor_tensor(dst, dst, tmp, ALU.subtract))

            R = [route[:, i, :] for i in range(6)]
            dve.wait_ge(s_end, ONE + 2 * BATCH)
            link(nc.vector.tensor_scalar(R[0], keys[:, :], rb_sb[:, 0:1], None, ALU.add))
            floor(R[1], R[0], R[2], route_i[:, :])
            link(nc.vector.tensor_scalar(R[3], R[1], 1.0 / EXPERTS, None, ALU.mult))
            floor(R[4], R[3], R[2], route_i[:, :])
            link(nc.vector.tensor_scalar(R[4], R[4], -float(EXPERTS), None, ALU.mult))
            link(nc.vector.tensor_tensor(R[5], R[1], R[4], ALU.add))
            link(nc.vector.tensor_tensor(onehot[:, 0:EXPERTS - 1, :], R[5].unsqueeze(1).broadcast_to([P, EXPERTS - 1, TILES]),
                                         iota[:, 0:EXPERTS - 1].unsqueeze(2).broadcast_to([P, EXPERTS - 1, TILES]), ALU.is_equal))
            link(nc.vector.tensor_tensor(R[0], onehot[:, 0, :], onehot[:, 1, :], ALU.add))
            link(nc.vector.tensor_tensor(R[0], R[0], onehot[:, 2, :], ALU.add))
            nc.vector.tensor_scalar(onehot[:, EXPERTS - 1, :], R[0], -1.0, 1.0, ALU.mult, ALU.add).then_inc(s_oh, 1)

            dve.wait_ge(s_rank, 1)
            per_tile = bank[0][:, EXPERTS * TILES:2 * EXPERTS * TILES].rearrange("p (e t) -> p e t", e=EXPERTS)
            in_tile = bank[0][:, 0:EXPERTS * TILES].rearrange("p (e t) -> p e t", e=EXPERTS)
            link(nc.vector.tensor_copy(count_a[:, :, :], per_tile))
            src, dst, k = count_a, count_b, 1
            while k < TILES:
                nc.vector.tensor_copy(dst[:, :, 0:k], src[:, :, 0:k])
                link(nc.vector.tensor_tensor(dst[:, :, k:TILES], src[:, :, k:TILES], src[:, :, 0:TILES - k], ALU.add))
                src, dst, k = dst, src, 2 * k
            total = src[:, :, TILES - 1]
            S = [small[:, i, :] for i in range(6)]
            link(nc.vector.tensor_scalar(S[0], total, float(P - 1), 1.0 / P, ALU.add, ALU.mult))
            floor(S[1], S[0], S[2], small_i[:, :])
            link(nc.vector.memset(S[3], 0.0))
            for e in range(1, EXPERTS):
                link(nc.vector.tensor_tensor(S[3][:, e:e + 1], S[3][:, e - 1:e], S[1][:, e - 1:e], ALU.add))
            link(nc.vector.tensor_scalar(S[4], S[3], float(P), None, ALU.mult))
            link(nc.vector.tensor_tensor(dst[:, :, :], src[:, :, :], per_tile, ALU.subtract))
            link(nc.vector.tensor_tensor(dst[:, :, :], dst[:, :, :], in_tile, ALU.add))
            link(nc.vector.tensor_tensor(dst[:, :, :], dst[:, :, :], S[4].unsqueeze(2).broadcast_to([P, EXPERTS, TILES]), ALU.add))
            link(nc.vector.tensor_tensor(dst[:, :, :], dst[:, :, :], onehot[:, :, :], ALU.mult))
            link(nc.vector.tensor_tensor(R[0], dst[:, 0, :], dst[:, 1, :], ALU.add))
            link(nc.vector.tensor_tensor(R[1], dst[:, 2, :], dst[:, 3, :], ALU.add))
            link(nc.vector.tensor_tensor(R[2], R[0], R[1], ALU.add))
            link(nc.vector.tensor_scalar(R[3], R[2], 1.0 / P, None, ALU.mult))
            floor(R[4], R[3], R[5], route_i[:, :])
            link(nc.vector.tensor_scalar(R[3], R[4], -float(P), None, ALU.mult))
            link(nc.vector.tensor_tensor(R[5], R[2], R[3], ALU.add))
            link(nc.vector.tensor_tensor(in_col[:, :, :], tile_no[:, :].unsqueeze(1).broadcast_to([P, TILES, SORTED]),
                                         R[4].unsqueeze(2).broadcast_to([P, TILES, SORTED]), ALU.is_equal))
            for n in range(2):
                nc.vector.tensor_tensor(pick[:, :, n, :], in_col[:, :, :],
                                        token_no[:, n, :].unsqueeze(2).broadcast_to([P, TILES, SORTED]), ALU.mult)
            for t in range(0, TILES, PICKS):
                nc.vector.tensor_tensor(sel[:, t:t + PICKS, :], iota[:, :].unsqueeze(1).broadcast_to([P, PICKS, P]),
                                        R[5][:, t:t + PICKS].unsqueeze(2).broadcast_to([P, PICKS, P]), ALU.is_equal).then_inc(s_sel, 1)
            T0, T1 = tile_e[:, 0, :], tile_e[:, 1, :]
            link(nc.vector.tensor_scalar(T0, tile_no[:, :], S[3][:, 1:2], None, ALU.is_ge))
            for e in range(2, EXPERTS):
                link(nc.vector.tensor_scalar(T1, tile_no[:, :], S[3][:, e:e + 1], None, ALU.is_ge))
                link(nc.vector.tensor_tensor(T0, T0, T1, ALU.add))
            nc.vector.tensor_copy(expert_of[:, :], T0).then_inc(s_eof, 1)
            dve.wait_ge(s_sum, 1)
            link(nc.vector.tensor_scalar(T1, bank[0][:, 0:SORTED], float(NO_TOKEN), None, ALU.add))
            link(nc.vector.tensor_tensor(T1, T1, bank[0][:, SORTED:2 * SORTED], ALU.add))
            nc.vector.tensor_copy(token_of[:, :], T1).then_inc(s_ids, 1)

            dve.wait_ge(s_eof, 1)
            dve.wait_ge(s_b1in, 16)

            def expert(j):
                return dve.value_load(expert_of[0:1, bass.ds(j, 1)], min_val=0, max_val=EXPERTS - 1)

            def add_b1(j):
                e = expert(j)
                for n in range(2):
                    dve.wait_ge(s_h, 2 * j + n + 1)
                    nc.vector.tensor_tensor(hid[:, n * 512:(n + 1) * 512], bank[1 + n][:, :], b1_sb[:, e, n * 512:(n + 1) * 512], ALU.add).then_inc(s_hb, 1)

            def end_tile(j):
                e = expert(j)
                dve.wait_ge(s_y, j + 1)
                nc.vector.tensor_tensor(z_a, bank[5][:, 0:E], vec[:, e + VECS.index("b2_0"), :], ALU.add).then_inc(s_yb, 1)
                dve.wait_ge(s_yb, ONE + j + 1)
                dve.wait_ge(s_xr, 16 * (j + 1))
                nc.vector.tensor_tensor(z_b, z_a, xr, ALU.add).then_inc(s_yr, 1)
                dve.wait_ge(s_yr, j + 1)
                layer_norm(3 * BATCH + j, lambda t: z_b, lambda t: z_a, 1)
                dve.wait_ge(s_ln, ONE + 3 * BATCH + j + 1)
                nc.vector.tensor_tensor(z_b, z_a, V["ln2g"], ALU.mult).then_inc(s_f1, 1)
                dve.wait_ge(s_f1, j + 1)
                nc.vector.tensor_tensor(z_c, z_b, V["ln2b"], ALU.add).then_inc(s_f2, 1)
                dve.wait_ge(s_f2, j + 1)
                dve.wait_ge(s_x1g, 16 * (j + 1))
                if not (isinstance(j, int) and j == 0):
                    dve.wait_ge(s_zst, 16 * j)
                nc.vector.tensor_tensor(z_out, z_c, x1g, ALU.add).then_inc(s_z, 1)

            add_b1(0)
            add_b1(1)
            end_tile(0)
            with dve.Fori(1, SORTED - 1) as j:
                add_b1(j + 1)
                end_tile(j)
            end_tile(SORTED - 1)


def kernel(**inputs):
    import concourse.bacc as bacc
    from concourse.bass_utils import run_bass_kernel_spmd

    I = {k: np.asarray(v) for k, v in inputs.items()}
    x0, f = "L0_xattn_", "L0_ffn_"

    def by_dim(w):
        return w.reshape(E, HEADS, HD).transpose(0, 2, 1).reshape(E, E)

    w_attn = np.stack([
        by_dim(I[x0 + "Wq"].T), by_dim(I[x0 + "Wk"].T), I[x0 + "Wv"].T, I[x0 + "Wo"].T,
        by_dim(I[f + "Wq"]), by_dim(I[f + "Wk"]), I[f + "Wv"], I[f + "Wo"],
    ])
    vec = np.stack([
        I[x0 + "bo"], I[f + "bv"], I[f + "bo"], I[f + "ln1_g"], I[f + "ln1_b"], I[f + "ln2_g"], I[f + "ln2_b"],
        I[f + "router_w"][:, 0], *I[f + "b2"],
    ])
    bias_qk = np.stack([I[f + n].reshape(HEADS, HD).T.reshape(KC, P) for n in ("bq", "bk")])
    arrays = {
        "x": I["x"].reshape(BATCH * SEQ, E),
        "ctx": I["ctx_1024"].reshape(BATCH * SEQ, E),
        "mask": I["mask_BxSxS2_bf1"].reshape(BATCH * SEQ, SEQ).view(np.uint8),
        "pad": I["mask_BxS2_bf1"].view(np.uint8).reshape(BATCH * TT, P).T,
        "w_attn": w_attn,
        "vec": vec,
        "bias_qk": bias_qk.transpose(2, 0, 1),
        "b1": I[f + "b1"],
        "tri_ones": np.stack([np.triu(np.ones((P, P), np.float32), 1), np.ones((P, P), np.float32)], 1),
        "tile_no": np.arange(SORTED, dtype=np.float32),
        "iota": np.arange(P, dtype=np.float32),
        "token_no": np.stack([np.tile(np.arange(TILES, dtype=np.float32) * P - NO_TOKEN, (P, 1)),
                              np.tile(np.arange(P, dtype=np.float32)[:, None], (1, TILES))], 1),
        "rb": I[f + "router_b"],
        "w1": I[f + "W1"],
        "w2": I[f + "W2"],
        "ident": np.eye(P, dtype=np.float32),
    }
    nc = bacc.Bacc("TRN2", target_bir_lowering=False, num_devices=1)
    io, given = {}, {}
    for name, a in arrays.items():
        a = np.ascontiguousarray(a)
        given[f"in_{name}"] = a
        io[name] = nc.dram_tensor(f"in_{name}", a.shape, mybir.dt.from_np(a.dtype), kind="ExternalInput").ap()
    io["out"] = nc.dram_tensor("out_x", (BATCH * SEQ, E), F32, kind="ExternalOutput").ap()
    build(nc, io)
    r = run_bass_kernel_spmd(nc, [given], core_ids=[0])
    return r.results[0]["out_x"].reshape(BATCH, SEQ, E)
```
